# Optimizing a Trainium2 kernel written in Bass

```python
import numpy as np
import jax
import jax.numpy as jnp

def _softmax(x, axis=-1):
    return jax.nn.softmax(x, axis=axis)

def _gelu(x):
    return jax.nn.gelu(x, approximate=True)

def _silu(x):
    return jax.nn.silu(x)

def _sigmoid(x):
    return jax.nn.sigmoid(x)

def _layernorm(x, axis=-1, eps=1e-05):
    m = jnp.mean(x, axis=axis, keepdims=True)
    v = jnp.var(x, axis=axis, keepdims=True)
    return (x - m) / jnp.sqrt(v + eps)

def _scatter_add(tgt, idx, src, axis=0):
    return tgt.at[idx].add(src)

def _segment_sum(src, seg, n):
    return jax.ops.segment_sum(src, seg, n)
kernel_name = 'mk_adj_preln_d2_adj_r2_3a23d5'

def setup_inputs(seed: int=0):
    np.random.seed(seed)
    _w = jnp.asarray

    def _rec_inputs():
        import jax
        import jax.numpy as jnp
        _gk = jax.random.key(seed)
        x = -0.000929 + 1 * jax.random.normal(jax.random.fold_in(_gk, 1), (4096, 128), jnp.float32)
        _a = jax.random.bernoulli(jax.random.fold_in(_gk, 2), 0.00390625, (4096, 4096))
        _a = jnp.logical_or(_a, jnp.eye(4096, dtype=bool))
        _af = _a.astype(jnp.float32)
        adj = _af
        return (x, adj)
    x, adj = _rec_inputs()

    def _L0_gnn_setup():
        import jax, jax.numpy as jnp
        import numpy as np
        N, DIN, DOUT = (4096, 128, 128)
        NEG = -9000000000000000.0
        ALPHA = 0.2
        key = jax.random.key(seed)
        kx, ka, kw, ks, kr = jax.random.split(key, 5)
        X = jax.random.normal(kx, (N, DIN), dtype=jnp.float32)
        A = (jax.random.uniform(ka, (N, N)) < 0.01).astype(jnp.float32)
        A = A.at[jnp.arange(N), jnp.arange(N)].set(1.0)
        lim_w = float(np.sqrt(6.0 / (DIN + DOUT)))
        W = jax.random.uniform(kw, (DOUT, DIN), jnp.float32, -lim_w, lim_w)
        b = jnp.zeros((DOUT,), jnp.float32)
        lim_a = float(np.sqrt(6.0 / (DOUT + 1)))
        a_s = jax.random.uniform(ks, (DOUT, 1), jnp.float32, -lim_a, lim_a)
        a_r = jax.random.uniform(kr, (DOUT, 1), jnp.float32, -lim_a, lim_a)
        return {'X': X, 'A': A, 'W': W, 'b': b, 'a_s': a_s, 'a_r': a_r}
    _L0_gnn_all = _L0_gnn_setup()
    _L0_gnn_in = {k: v for k, v in _L0_gnn_all.items() if k in ('W', 'b', 'a_s', 'a_r')}
    del _L0_gnn_all

    def _L1_gnn_setup():
        import jax, jax.numpy as jnp
        import numpy as np
        N, D = (4096, 128)
        EDGE_PROB = 0.005
        COS_EPS = 1e-08
        key = jax.random.key(seed)
        kx, ka = jax.random.split(key)
        x = jax.random.normal(kx, (N, D), dtype=jnp.float32)
        adj = (jax.random.uniform(ka, (N, N)) < EDGE_PROB).astype(jnp.float32)
        return {'t': jnp.float32(0.0), 'x': x, 'adj': adj, 'alpha': jnp.float32(0.5), 'beta': jnp.float32(1.0)}
    _L1_gnn_all = _L1_gnn_setup()
    _L1_gnn_in = {k: v for k, v in _L1_gnn_all.items() if k in ('t', 'alpha', 'beta')}
    del _L1_gnn_all
    return {'x': x, 'adj': adj, 'L0_gnn_W': _L0_gnn_in['W'], 'L0_gnn_b': _L0_gnn_in['b'], 'L0_gnn_a_s': _L0_gnn_in['a_s'], 'L0_gnn_a_r': _L0_gnn_in['a_r'], 'L1_gnn_t': _L1_gnn_in['t'], 'L1_gnn_alpha': _L1_gnn_in['alpha'], 'L1_gnn_beta': _L1_gnn_in['beta']}

def reference(x, adj, L0_gnn_W, L0_gnn_b, L0_gnn_a_s, L0_gnn_a_r, L1_gnn_t, L1_gnn_alpha, L1_gnn_beta):
    import jax
    import jax.numpy as jnp

    def _L0_gnn_ref(X, A, W, b, a_s, a_r):
        import jax, jax.numpy as jnp
        import numpy as np
        N, DIN, DOUT = (4096, 128, 128)
        NEG = -9000000000000000.0
        ALPHA = 0.2
        H = X @ W.T + b
        s = H @ a_s
        r = H @ a_r
        e = jax.nn.leaky_relu(A * s + A * r.T, negative_slope=ALPHA)
        masked = jnp.where(A > 0, e, NEG)
        att = jax.nn.softmax(masked, axis=1)
        H_out = att @ H
        return H_out

    def _L1_gnn_ref(t, x, adj, alpha, beta):
        import jax, jax.numpy as jnp
        import numpy as np
        N, D = (4096, 128)
        EDGE_PROB = 0.005
        COS_EPS = 1e-08
        deg = jnp.clip(adj.sum(axis=1), 1.0)
        dis = deg ** (-0.5)
        adj_norm = dis[:, None] * adj * dis[None, :]
        diffusion = adj_norm @ x - x
        norms = jnp.maximum(jnp.linalg.norm(x, axis=-1), COS_EPS)
        sim = x @ x.T / (norms[:, None] * norms[None, :])
        attn = jax.nn.softmax(beta * sim * adj, axis=1)
        attn = jax.lax.stop_gradient(attn)
        return diffusion + jax.nn.sigmoid(alpha) * (attn @ x - x)
    h = jnp.maximum(_layernorm(x, axis=-1), 0.0)
    x = x + _L0_gnn_ref(h, adj, L0_gnn_W, L0_gnn_b, L0_gnn_a_s, L0_gnn_a_r)
    h = jnp.maximum(_layernorm(x, axis=-1), 0.0)
    x = x + _L1_gnn_ref(L1_gnn_t, h, adj, L1_gnn_alpha, L1_gnn_beta)
    return x

_drawn_inputs = setup_inputs


def setup_inputs(seed=0):
    import zlib

    import numpy as np

    out = dict(_drawn_inputs(seed))
    spreads = {'L0_gnn_b': (0.0, 0.1)}
    factors = {}
    for name, (base, spread) in spreads.items():
        noise = np.random.default_rng([zlib.crc32(name.encode()), seed]).standard_normal(out[name].shape)
        drawn = base * np.exp(spread * noise) if base else spread * noise
        out[name] = jnp.asarray(drawn.astype(out[name].dtype))
    for name, factor in factors.items():
        out[name] = (out[name] * factor).astype(out[name].dtype)
    return out
```

```python
from contextlib import ExitStack

import concourse.bass as bass
from concourse import mybir

ALU = mybir.AluOpType
ACT = mybir.ActivationFunctionType
F32 = mybir.dt.float32
F16 = mybir.dt.float16
BF16 = mybir.dt.bfloat16
U8 = mybir.dt.uint8
AX = mybir.AxisListType

P = 128
SLOPE = 0.2
LN_EPS = 1e-5
COS_EPS = 1e-8
HN_SCALE = 256.0
DH_SCALE = 1024.0


def gat_then_cosine_diffusion(nc, x, adjT, W, WT, a_s_cols, a_r, a_s, b_rows, b_cols, alpha, beta, out):
    N, D = x.shape
    T = N // P
    CW = 1024
    C = N // CW
    R = CW // P
    A = D + 1
    BK = 3
    NT = C * T
    SLOTS = 4
    ASLOTS = 4
    assert D == P and N == C * CW

    def bank(r):
        return r // BK, (r % BK) * A

    BANKS = [(k, min(BK, R - BK * k)) for k in range((R + BK - 1) // BK)]

    with ExitStack() as ctx:
        def sb(name, shape, dt=F32):
            return ctx.enter_context(nc.sbuf_tensor(name, shape, dt))

        def sem(name):
            return ctx.enter_context(nc.semaphore(name))

        adj8 = sb("adj8", [P, NT, CW], U8)
        stage = sb("stage", [P, SLOTS, CW])
        cbuf = sb("cbuf", [P, T * A])
        gbuf = sb("gbuf", [P, T, A])
        res = sb("res", [P, T, D])
        wt = sb("wt", [P, 2, CW])
        ident = sb("ident", [P, P])
        ones = sb("ones", [P, P])
        pair = sb("pair", [P, CW], BF16)
        ones16 = sb("ones16", [P, 2], BF16)
        zeros = sb("zeros", [P, P], F16)
        tot = sb("tot", [P, A])
        bst = sb("bst", [P, R, 6])
        mv = sb("mv", [P, T, 2])
        rin = sb("rin", [P, T])
        rout = sb("rout", [P, T])
        half = sb("half", [P, T])
        dis = sb("dis", [P, T])
        disd = sb("disd", [P, T])
        vj = sb("vj", [P, T])
        gj = sb("gj", [P, T])
        rden = sb("rden", [P, R])
        sc = sb("sc", [P, 24])

        (C_RMAX, C_RTOP, C_M8R, C_M2R, C_MBS, C_BAS, C_EMA, C_SIG, C_MSIG, C_BETA, C_ALPHA,
         C_BSC, C_NB, C_E0, C_AS, C_T) = range(16)

        def col(k):
            return sc[:, k:k + 1]

        cb = cbuf[:, 0:N]
        h1a = cbuf[:, :].rearrange("p (t a) -> p t a", a=A)
        h1 = h1a[:, :, 0:D]
        late = adj8[:, NT - T:NT, :].rearrange("p n i -> p (n i)").bitcast(F32)
        h0 = late[:, 0:T * D].rearrange("p (t d) -> p t d", d=D)
        h0T = late[:, T * D:2 * T * D]
        LATE = NT - T - 4
        wk = adj8[:, LATE:NT - T, :].rearrange("p n i -> p (n i)").bitcast(F32)
        w_sb, as_sb, bc_sb = wk[:, 0:128], wk[:, 128:256], wk[:, 256:384]
        ar_as = wk[:, 384:386]
        brow = wk[:, 386:386 + A]
        wtr = wk[:, 520:520 + A]
        ws_sb = wk[:, 652:652 + P]
        hn = stage[:, :, :].rearrange("p s i -> p (s i)").rearrange("p (t d) -> p t d", d=D)
        dh = stage[:, :, :].rearrange("p s i -> p (s i)").bitcast(F16).rearrange("p (t k d) -> p t k d", k=2, d=D)
        a16 = wt[:, :, :].rearrange("p s i -> p (s i)").bitcast(BF16).rearrange("p (s i) -> p s i", s=ASLOTS)
        hnT = gbuf[:, :, :].rearrange("p t a -> p (t a)")[:, 0:N].bitcast(F16).rearrange("p (k i) -> p k i", k=2)
        fin = stage[:, 2:4, :].rearrange("p s i -> p (s i)")[:, 0:R * A].rearrange("p (r a) -> p r a", a=A)

        ps = ctx.enter_context(nc.psum_tensor("ps", [P, 8, 512], F32))
        zb = ps[:, 0:4, :]
        acc = ps[:, 4:7, :]
        misc = ps[:, 7, :]

        def area(k):
            return zb[:, 2 * k:2 * k + 2, :].rearrange("p b i -> p (b i)")

        def accs(k, n):
            return acc[:, k, 0:n * A].rearrange("p (r a) -> p r a", a=A)

        x_loaded = [sem(f"x_loaded{q}") for q in range(C)]
        w_loaded = sem("w_loaded")
        stage_loaded = [sem(f"stage_loaded{s}") for s in range(SLOTS)]
        adj_kept = sem("adj_kept")
        consts_ready = sem("consts_ready")
        rsqrt_asked = sem("rsqrt_asked")
        rsqrt_done = sem("rsqrt_done")
        dve_step = sem("dve_step")
        act_step = sem("act_step")
        wprod_ready = sem("wprod_ready")
        wprod_kept = sem("wprod_kept")
        h0_ready = sem("h0_ready")
        h0T_psum = sem("h0T_psum")
        h0T_ready = sem("h0T_ready")
        H_psum = sem("H_psum")
        H_kept = sem("H_kept")
        s_psum = sem("s_psum")
        s_kept = sem("s_kept")
        rmax_part = sem("rmax_part")
        rmax_row = sem("rmax_row")
        rmax_one = sem("rmax_one")
        rmax_all = sem("rmax_all")
        shift_ready = sem("shift_ready")
        vg_ready = sem("vg_ready")
        c_raw = sem("c_raw")
        scal_ready = sem("scal_ready")
        g_ready = sem("g_ready")
        p_ready = sem("p_ready")
        p_used = sem("p_used")
        rden_ready = sem("rden_ready")
        acc_free = sem("acc_free")
        hn_ready = sem("hn_ready")
        hnT_psum = sem("hnT_psum")
        hnT_hi = sem("hnT_hi")
        hnT_lo = sem("hnT_lo")
        tot_psum = sem("tot_psum")
        dtmp_ready = sem("dtmp_ready")
        dh_hi = sem("dh_hi")
        dh_lo = sem("dh_lo")
        pair_ready = sem("pair_ready")
        pair_used = sem("pair_used")
        a16_ready = sem("a16_ready")
        a16_used = sem("a16_used")
        d_free = sem("d_free")
        d_low = sem("d_low")
        z_ready = sem("z_ready")
        q_ready = sem("q_ready")
        y_ready = sem("y_ready")
        y_used = sem("y_used")
        fin_ready = sem("fin_ready")
        out_ready = sem("out_ready")
        stored = sem("stored")

        xt = x.rearrange("(t p) d -> p t d", p=P)
        ot = out.rearrange("(t p) d -> p t d", p=P)
        at = adjT.rearrange("(t p) (c i) -> c t p i", p=P, i=CW)

        block = ctx.enter_context(nc.Block())

        @block.sync
        def _(sp):
            def load(c, g, waits):
                for s in range(SLOTS):
                    if waits:
                        sp.wait_ge(adj_kept, c * T + g * SLOTS + s - (SLOTS - 1))
                    sp.dma_start(stage[:, s, :], at[c, g * SLOTS + s]).then_inc(stage_loaded[s], 16)

            load(0, 0, False)
            with sp.Fori(1, T // SLOTS) as g:
                load(0, g, True)
            with sp.Fori(1, C) as c:
                with sp.Fori(0, T // SLOTS) as g:
                    load(c, g, True)
            for c in range(C):
                sp.wait_ge(out_ready, c + 1)
                sp.dma_start(ot[:, c * R:(c + 1) * R, :], res[:, c * R:(c + 1) * R, :]).then_inc(stored, 16)
            sp.wait_ge(stored, 16 * C)

        @block.gpsimd
        def _(pool):
            pool.memset(ident[:, :], 0.0).then_inc(consts_ready, 1)
            pool.memset(ones[:, :], 1.0).then_inc(consts_ready, 1)
            pool.memset(half[:, :], -0.5).then_inc(consts_ready, 1)
            pool.memset(ones16[:, :], 1.0).then_inc(consts_ready, 1)
            pool.memset(zeros[:, :], 0.0).then_inc(consts_ready, 1)
            pool.wait_ge(consts_ready, 5)
            pool.affine_select(out=ident[:, :], in_=ident[:, :], compare_op=ALU.not_equal, fill=1.0, base=0,
                               pattern=[[-1, P]], channel_multiplier=1).then_inc(consts_ready, 1)
            done = 0
            for norm in ("ln0", "ln1"):
                for q in range(C):
                    pool.wait_ge(rsqrt_asked, done + 1)
                    w = slice(q * R, (q + 1) * R)
                    nc.gpsimd.tensor_tensor(rout[:, w], rin[:, w], half[:, w], ALU.pow).then_inc(rsqrt_done, 1)
                    done += 1
            pool.wait_ge(rsqrt_asked, done + 1)
            nc.gpsimd.tensor_tensor(dis[:, :], rin[:, :], half[:, :], ALU.pow).then_inc(rsqrt_done, 1)
            pool.wait_ge(rsqrt_asked, done + 2)
            nc.gpsimd.tensor_tensor(rout[:, :], rin[:, :], half[:, :], ALU.pow).then_inc(rsqrt_done, 1)

        @block.scalar
        def _(act):
            for q in range(C):
                act.dma_start(res[:, q * R:(q + 1) * R, :], xt[:, q * R:(q + 1) * R, :]).then_inc(x_loaded[q], 16)
                if q == 0:
                    act.dma_start(w_sb, W).then_inc(w_loaded, 16)
                    act.dma_start(wtr[:, 0:D], WT).then_inc(w_loaded, 16)
                    act.dma_start(as_sb, a_s_cols).then_inc(w_loaded, 16)
                    act.dma_start(bc_sb, b_cols).then_inc(w_loaded, 16)
                    act.dma_start(brow[:, 0:D], b_rows).then_inc(w_loaded, 16)
                    act.dma_start(ar_as[:, 0:1], a_r).then_inc(w_loaded, 16)
                    act.dma_start(ar_as[:, 1:2], a_s).then_inc(w_loaded, 16)
                    act.dma_start(col(C_ALPHA), alpha).then_inc(w_loaded, 16)
                    act.dma_start(col(C_BETA), beta).then_inc(w_loaded, 16)

            act.wait_ge(wprod_ready, 1)
            nc.scalar.activation(ws_sb, misc[:, 0:P], ACT.Copy).then_inc(wprod_kept, 1)
            nc.scalar.activation(wtr[:, D:A], misc[:, 128:129], ACT.Copy).then_inc(wprod_kept, 1)
            nc.scalar.activation(brow[:, D:A], misc[:, 130:131], ACT.Copy).then_inc(wprod_kept, 1)
            nc.scalar.activation(col(C_BAS), misc[:, 131:132], ACT.Copy).then_inc(wprod_kept, 1)
            for q in range(C):
                w = slice(q * CW, (q + 1) * CW)
                act.wait_ge(h0T_psum, q + 1)
                nc.scalar.activation(h0T[:, w], area(q % 2), ACT.Copy).then_inc(h0T_ready, 1)
                act.wait_ge(s_psum, q + 1)
                nc.scalar.activation(cb[:, w], area(q % 2), ACT.Copy).then_inc(s_kept, 1)
            act.wait_ge(w_loaded, 16 * 9)
            nc.scalar.activation(col(C_EMA), col(C_ALPHA), ACT.Exp, scale=-1.0).then_inc(scal_ready, 1)
            act.wait_ge(shift_ready, 1)
            nc.scalar.activation(vj[:, :], gbuf[:, :, D], ACT.Exp, bias=col(C_M8R), scale=1 - SLOPE).then_inc(vg_ready, 1)
            nc.scalar.activation(gj[:, :], gbuf[:, :, D], ACT.Exp, bias=col(C_M2R), scale=SLOPE).then_inc(vg_ready, 1)
            act.wait_ge(s_kept, C)
            for q in range(C):
                w = slice(q * CW, (q + 1) * CW)
                nc.scalar.activation(cb[:, w], cb[:, w], ACT.Exp, bias=col(C_MBS), scale=-(1 - SLOPE)).then_inc(c_raw, 1)
            nc.scalar.activation(col(C_E0), col(C_NB), ACT.Exp).then_inc(scal_ready, 1)

            def keep(g):
                for s in range(SLOTS):
                    act.wait_ge(stage_loaded[s], 16 * g + 16)
                    nc.scalar.activation(adj8[:, g * SLOTS + s, :], stage[:, s, :],
                                         ACT.Copy).then_inc(adj_kept, 1)

            with act.Fori(0, LATE // SLOTS) as g:
                keep(g)
            act.wait_ge(g_ready, 1)
            with act.Fori(LATE // SLOTS, NT // SLOTS) as g:
                keep(g)

            for q in range(C):
                act.wait_ge(hnT_psum, q + 1)
                nc.scalar.activation(hnT[:, 0, q * CW:(q + 1) * CW], area(q % 2), ACT.Copy).then_inc(hnT_hi, 1)
            for q in range(C):
                act.wait_ge(dtmp_ready, q + 1)
                nc.scalar.activation(dh[:, q * R:(q + 1) * R, 0, :],
                                     wt[:, q % 2, :].rearrange("p (t d) -> p t d", d=D),
                                     ACT.Copy).then_inc(dh_hi, 1)

            act.wait_ge(a16_used, NT)

            def weight(n, par, waits):
                act.wait_ge(z_ready, n + 1)
                if waits:
                    act.wait_ge(y_ready, n - 1)
                nc.scalar.activation(stage[:, par, :], area(par), ACT.Exp, bias=col(C_NB),
                                     scale=col(C_BSC)).then_inc(q_ready, 1)

            weight(0, 0, False)
            weight(1, 1, False)
            with act.Fori(1, NT // 2) as k:
                weight(2 * k, 0, True)
                weight(2 * k + 1, 1, True)

        @block.tensor
        def _(pe):
            pe.wait_ge(w_loaded, 16 * 9)
            pe.matmul(misc[:, 0:P], w_sb, as_sb, start=True, stop=True)
            pe.matmul(misc[:, 128:129], w_sb, ar_as[:, 0:1], start=True, stop=True)
            pe.matmul(misc[:, 130:132], bc_sb, ar_as, start=True, stop=True).then_inc(wprod_ready, 1)
            pe.wait_ge(consts_ready, 6)
            for q in range(C):
                pe.wait_ge(h0_ready, q + 1)
                if q >= 2:
                    pe.wait_ge(s_kept, q - 1)
                for t in range(R):
                    mm = pe.transpose(area(q % 2)[:, t * P:(t + 1) * P], h0[:, q * R + t, :], ident[:, :])
                mm.then_inc(h0T_psum, 1)
                pe.wait_ge(h0T_ready, q + 1)
                if q == 0:
                    pe.wait_ge(wprod_kept, 4)
                if q >= 1:
                    pe.wait_ge(H_kept, q)
                for t in range(R):
                    k, o = bank(t)
                    mm = pe.matmul(acc[:, k, o:o + A], h0T[:, (q * R + t) * P:(q * R + t + 1) * P], wtr,
                                   start=True, stop=True)
                mm.then_inc(H_psum, 1)
                for f in range(CW // 512):
                    mm = pe.matmul(zb[:, 2 * (q % 2) + f, :], ws_sb,
                                   h0T[:, q * CW + f * 512:q * CW + (f + 1) * 512], start=True, stop=True)
                mm.then_inc(s_psum, 1)
            pe.wait_ge(rmax_part, 1)
            pe.transpose(misc[0:1, 256:256 + P], col(C_RMAX), ident[:, :]).then_inc(rmax_row, 1)
            pe.wait_ge(rmax_one, 1)
            pe.matmul(misc[:, 400:401], ones[0:1, :], sc[0:1, C_RTOP:C_RTOP + 1],
                      start=True, stop=True).then_inc(rmax_all, 1)

            pe.wait_ge(g_ready, 1)
            pe.matmul(misc[:, 0:T], zeros[:, :], zeros[:, 0:T], start=True, stop=False, skip_group_check=True)

            def attend(c, k, first):
                for par in range(2):
                    n = c * T + 2 * k + par
                    pe.wait_ge(p_ready, n + 1)
                    for r in range(R):
                        b, o = bank(r)
                        mm = pe.matmul(acc[:, b, o:o + A], wt[:, par, r * P:(r + 1) * P], gbuf[:, 2 * k + par, :],
                                       start=first and par == 0 and r % BK == 0, stop=False, skip_group_check=True)
                    mm.then_inc(p_used, 1)
                pe.wait_ge(pair_ready, c * (T // 2) + k + 1)
                for r in range(R):
                    mm = pe.matmul(misc[:, bass.ds(c * R + r, 1)], pair[:, r * P:(r + 1) * P], ones16[:, 0:1],
                                   start=False, stop=False, skip_group_check=True)
                mm.then_inc(pair_used, 1)

            with pe.Fori(0, C) as c:
                pe.wait_ge(acc_free, c + 1)
                attend(c, 0, True)
                with pe.Fori(1, T // 2) as k:
                    attend(c, k, False)

            for q in range(C):
                pe.wait_ge(hn_ready, q + 1)
                if q >= 2:
                    pe.wait_ge(hnT_lo, q - 1)
                for t in range(R):
                    mm = pe.transpose(area(q % 2)[:, t * P:(t + 1) * P], hn[:, q * R + t, :], ident[:, :])
                mm.then_inc(hnT_psum, 1)
            for t in range(T):
                mm = pe.matmul(acc[:, 2, 0:A], ones[:, :], h1a[:, t, :], start=(t == 0), stop=(t == T - 1))
            mm.then_inc(tot_psum, 1)

            pe.wait_ge(dh_lo, C)

            def diffuse(c, t, slot, area_no, first):
                n = c * T + t
                pe.wait_ge(a16_ready, n + 1)
                for r in range(R):
                    mm = pe.matmul(ps[:, 4 * area_no + r // 2, (r % 2) * 2 * D:(r % 2 + 1) * 2 * D],
                                   a16[:, slot, r * P:(r + 1) * P], dh[:, t, :, :].rearrange("p k d -> p (k d)"),
                                   start=first and r % 2 == 0, stop=False, skip_group_check=True)
                mm.then_inc(a16_used, 1)

            with pe.Fori(0, C // 2) as c2:
                for half_no in range(2):
                    c = 2 * c2 + half_no
                    pe.wait_ge(d_free, 2 * c2 + 1)
                    for t in range(ASLOTS):
                        diffuse(c, t, t, half_no, t == 0)
                    with pe.Fori(1, T // ASLOTS) as g:
                        for s in range(ASLOTS):
                            diffuse(c, g * ASLOTS + s, s, half_no, False)

            def cosine(c, t, n, par, waits):
                if waits:
                    pe.wait_ge(q_ready, n - 1)
                for a, b in ((0, 0), (0, 1), (1, 0)):
                    for f in range(CW // 512):
                        mm = pe.matmul(zb[:, 2 * par + f, :], hnT[:, a, bass.ds(t * P, P)],
                                       hnT[:, b, bass.ds(c * CW + f * 512, 512)],
                                       start=(a, b) == (0, 0), stop=a == 1, skip_group_check=True)
                mm.then_inc(z_ready, 1)

            def weigh(t, n, par, first):
                pe.wait_ge(y_ready, n + 1)
                for r in range(R):
                    b, o = bank(r)
                    mm = pe.matmul(acc[:, b, o:o + A], wt[:, par, r * P:(r + 1) * P], h1a[:, t, :],
                                   start=first and r % BK == 0, stop=False, skip_group_check=True)
                mm.then_inc(y_used, 1)

            def chunk(c, last):
                n0 = c * T
                pe.wait_ge(acc_free, C + 1 + c)
                weigh(0, n0, 0, True)
                cosine(c, 2, n0 + 2, 0, True)
                weigh(1, n0 + 1, 1, False)
                cosine(c, 3, n0 + 3, 1, True)
                with pe.Fori(1, T // 2 - 1) as k:
                    weigh(2 * k, n0 + 2 * k, 0, False)
                    cosine(c, 2 * k + 2, n0 + 2 * k + 2, 0, True)
                    weigh(2 * k + 1, n0 + 2 * k + 1, 1, False)
                    cosine(c, 2 * k + 3, n0 + 2 * k + 3, 1, True)
                weigh(T - 2, n0 + T - 2, 0, False)
                if not last:
                    cosine(c + 1, 0, n0 + T, 0, True)
                weigh(T - 1, n0 + T - 1, 1, False)
                if not last:
                    cosine(c + 1, 1, n0 + T + 1, 1, True)

            pe.wait_ge(d_free, C + 1)
            cosine(0, 0, 0, 0, False)
            cosine(0, 1, 1, 1, False)
            with pe.Fori(0, C - 1) as c:
                chunk(c, False)
            chunk(C - 1, True)

        @block.vector
        def _(dve):
            steps = [0]
            asked = [0]

            def link(ins):
                steps[0] += 1
                ins.then_inc(dve_step, 1)
                dve.wait_ge(dve_step, steps[0])

            def rsqrt():
                dve.wait_ge(rsqrt_done, asked[0])

            def ask(ins):
                asked[0] += 1
                ins.then_inc(rsqrt_asked, 1)

            def layer_norm_relu(q, dst):
                w = slice(q * R, (q + 1) * R)
                for t in range(R):
                    ins = nc.vector.bn_stats(bst[:, t, :], res[:, q * R + t, :])
                link(ins)
                for t in range(R):
                    ins = nc.vector.bn_aggr(mv[:, q * R + t, :], bst[:, t, :])
                link(ins)
                ask(nc.vector.tensor_scalar(rin[:, w], mv[:, w, 1], LN_EPS, None, ALU.add))
                link(nc.vector.tensor_tensor(dst[:, w, :], res[:, w, :],
                                             mv[:, w, 0:1].broadcast_to([P, R, D]), ALU.subtract))
                rsqrt()
                return nc.vector.scalar_tensor_tensor(
                    out=dst[:, w, :], in0=dst[:, w, :], scalar=0.0,
                    in1=rout[:, w].unsqueeze(2).broadcast_to([P, R, D]), op0=ALU.max, op1=ALU.mult)

            def keep_H(q):
                dve.wait_ge(H_psum, q + 1)
                if q == 0:
                    dve.wait_ge(wprod_kept, 4)
                for k, n in BANKS:
                    t0 = q * R + k * BK
                    ins = nc.vector.tensor_tensor(gbuf[:, t0:t0 + n, :], accs(k, n),
                                                  brow.unsqueeze(1).broadcast_to([P, n, A]), ALU.add)
                ins.then_inc(H_kept, 1)

            for q in range(C):
                dve.wait_ge(x_loaded[q], 16)
                layer_norm_relu(q, h0).then_inc(h0_ready, 1)
                if q >= 1:
                    keep_H(q - 1)
            keep_H(C - 1)
            dve.wait_ge(H_kept, C)
            nc.vector.tensor_reduce(col(C_RMAX), gbuf[:, :, D], AX.X, ALU.max).then_inc(rmax_part, 1)
            dve.wait_ge(scal_ready, 1)
            link(nc.vector.tensor_scalar(col(C_T), col(C_EMA), 1.0, None, ALU.add))
            link(nc.vector.reciprocal(col(C_SIG), col(C_T)))
            nc.vector.tensor_scalar(col(C_MSIG), col(C_SIG), -1.0, -1.0, ALU.mult, ALU.add)
            nc.vector.tensor_scalar(col(C_BSC), col(C_BETA), 1.0 / HN_SCALE ** 2, None, ALU.mult)
            nc.vector.scalar_tensor_tensor(out=col(C_NB), in0=col(C_BETA), scalar=-1.0, in1=col(C_BETA),
                                           op0=ALU.mult, op1=ALU.min)
            dve.wait_ge(rmax_row, 1)
            nc.vector.tensor_reduce(sc[0:1, C_RTOP:C_RTOP + 1], misc[0:1, 256:256 + P], AX.X,
                                    ALU.max).then_inc(rmax_one, 1)
            dve.wait_ge(rmax_all, 1)
            nc.vector.tensor_scalar(col(C_M8R), misc[:, 400:401], -(1 - SLOPE), None, ALU.mult).then_inc(acc_free, 1)
            nc.vector.tensor_scalar(col(C_M2R), misc[:, 400:401], -SLOPE, None, ALU.mult)
            link(nc.vector.tensor_scalar(col(C_AS), col(C_BAS), -(1 - SLOPE), None, ALU.mult))
            nc.vector.tensor_tensor(col(C_MBS), col(C_AS), col(C_M8R), ALU.add).then_inc(shift_ready, 1)
            dve.wait_ge(vg_ready, 2)
            link(nc.vector.tensor_tensor(gbuf[:, :, 0:D], gbuf[:, :, 0:D],
                                         gj[:, :].unsqueeze(2).broadcast_to([P, T, D]), ALU.mult))
            nc.vector.tensor_copy(gbuf[:, :, D], gj[:, :])
            for q in range(C):
                dve.wait_ge(c_raw, q + 1)
                ins = nc.vector.tensor_scalar(cb[:, q * CW:(q + 1) * CW], cb[:, q * CW:(q + 1) * CW], 1.0, None, ALU.min)
            ins.then_inc(g_ready, 1)
            dve.wait_ge(g_ready, 1)

            def edge_weights(c, t, par, waits):
                n = c * T + t
                dve.wait_ge(adj_kept, n + 1)
                if waits:
                    dve.wait_ge(p_used, n - 1)
                nc.vector.scalar_tensor_tensor(out=wt[:, par, :], in0=cb[:, bass.ds(c * CW, CW)],
                                               scalar=vj[:, bass.ds(t, 1)], in1=adj8[:, n, :],
                                               op0=ALU.max, op1=ALU.mult).then_inc(p_ready, 1)

            def degree_pair(m, waits):
                if waits:
                    dve.wait_ge(pair_used, m)
                nc.vector.tensor_tensor(pair[:, :], adj8[:, 2 * m, :], adj8[:, 2 * m + 1, :],
                                        ALU.add).then_inc(pair_ready, 1)

            def add_attention(c):
                dve.wait_ge(p_used, c * T + T)
                for k, n in BANKS:
                    ins = nc.vector.reciprocal(rden[:, k * BK:k * BK + n], accs(k, n)[:, :, D])
                ins.then_inc(rden_ready, 1)
                dve.wait_ge(rden_ready, c + 1)
                for r in range(R):
                    b, o = bank(r)
                    row = res[:, bass.ds(c * R + r, 1), :].squeeze(1)
                    ins = nc.vector.scalar_tensor_tensor(out=row, in0=acc[:, b, o:o + D], scalar=rden[:, r:r + 1],
                                                         in1=row, op0=ALU.mult, op1=ALU.add)
                ins.then_inc(acc_free, 1)

            def edge_rest(c):
                with dve.Fori(1, T // 2) as k:
                    edge_weights(c, 2 * k, 0, True)
                    edge_weights(c, 2 * k + 1, 1, True)
                    degree_pair(c * (T // 2) + k, True)

            edge_weights(0, 0, 0, False)
            edge_weights(0, 1, 1, False)
            degree_pair(0, False)
            with dve.Fori(0, C - 1) as c:
                edge_rest(c)
                edge_weights(c + 1, 0, 0, True)
                edge_weights(c + 1, 1, 1, True)
                degree_pair((c + 1) * (T // 2), True)
                add_attention(c)
            edge_rest(C - 1)
            add_attention(C - 1)
            dve.wait_ge(acc_free, C + 1)

            for q in range(C):
                link(layer_norm_relu(q, h1))
            nc.vector.memset(h1a[:, :, D:A], 1.0)
            dve.wait_ge(pair_used, NT // 2)
            ask(nc.vector.tensor_scalar(rin[:, :], misc[:, 0:T], 1.0, None, ALU.max))
            link(nc.vector.tensor_tensor(hn[:, :, :], h1, h1, ALU.mult))
            link(nc.vector.tensor_reduce(mv[:, :, 0], hn[:, :, :], AX.X, ALU.add))
            rsqrt()
            ask(nc.vector.tensor_scalar(rin[:, :], mv[:, :, 0], COS_EPS ** 2, None, ALU.max))
            nc.vector.tensor_scalar(disd[:, :], dis[:, :], 1.0 / DH_SCALE, None, ALU.mult).then_inc(d_free, 1)
            rsqrt()
            link(nc.vector.tensor_scalar(rout[:, :], rout[:, :], HN_SCALE, None, ALU.mult))
            for q in range(C):
                w = slice(q * R, (q + 1) * R)
                nc.vector.tensor_tensor(hn[:, w, :], h1[:, w, :], rout[:, w].unsqueeze(2).broadcast_to([P, R, D]),
                                        ALU.mult).then_inc(hn_ready, 1)
            for q in range(C):
                dve.wait_ge(hnT_hi, q + 1)
                w = slice(q * CW, (q + 1) * CW)
                nc.vector.tensor_tensor(hnT[:, 1, w], area(q % 2), hnT[:, 0, w], ALU.subtract).then_inc(hnT_lo, 1)
            dve.wait_ge(hnT_psum, C)
            for q in range(C):
                w = slice(q * R, (q + 1) * R)
                tmp = wt[:, q % 2, :].rearrange("p (t d) -> p t d", d=D)
                link(nc.vector.tensor_tensor(tmp, h1[:, w, :], dis[:, w].unsqueeze(2).broadcast_to([P, R, D]), ALU.mult))
                nc.vector.tensor_scalar(tmp, tmp, DH_SCALE, None, ALU.mult).then_inc(dtmp_ready, 1)
                dve.wait_ge(dtmp_ready, q + 1)
                dve.wait_ge(dh_hi, q + 1)
                nc.vector.tensor_tensor(dh[:, w, 1, :], tmp, dh[:, w, 0, :], ALU.subtract).then_inc(dh_lo, 1)
            dve.wait_ge(scal_ready, 2)
            dve.wait_ge(tot_psum, 1)
            link(nc.vector.tensor_scalar(tot[:, :], acc[:, 2, 0:A], col(C_E0), None, ALU.mult))
            link(nc.vector.scalar_tensor_tensor(out=res[:, :, :], in0=h1, scalar=col(C_MSIG), in1=res[:, :, :],
                                                op0=ALU.mult, op1=ALU.add))

            def widen(n, slot, waits):
                if waits:
                    dve.wait_ge(a16_used, n - (ASLOTS - 1))
                nc.vector.tensor_copy(a16[:, slot, :], adj8[:, n, :]).then_inc(a16_ready, 1)

            def add_diffusion(c, half_no):
                dve.wait_ge(a16_used, c * T + T)
                for k in (1, 0):
                    for r in range(R):
                        row = res[:, bass.ds(c * R + r, 1), :].squeeze(1)
                        o = (r % 2) * 2 * D + k * D
                        ins = nc.vector.scalar_tensor_tensor(
                            out=row, in0=ps[:, 4 * half_no + r // 2, o:o + D], scalar=disd[:, bass.ds(c * R + r, 1)],
                            in1=row, op0=ALU.mult, op1=ALU.add)
                    ins.then_inc(d_low if k else d_free, 1)
                    if k:
                        dve.wait_ge(d_low, c + 1)

            def widen_rest(c):
                with dve.Fori(1, T // ASLOTS) as g:
                    for s in range(ASLOTS):
                        widen(c * T + g * ASLOTS + s, s, True)

            for s in range(ASLOTS):
                widen(s, s, False)
            with dve.Fori(0, C // 2 - 1) as c2:
                for half_no in range(2):
                    widen_rest(2 * c2 + half_no)
                    for s in range(ASLOTS):
                        widen((2 * c2 + half_no + 1) * T + s, s, True)
                    add_diffusion(2 * c2 + half_no, half_no)
            widen_rest(C - 2)
            for s in range(ASLOTS):
                widen((C - 1) * T + s, s, True)
            add_diffusion(C - 2, 0)
            widen_rest(C - 1)
            add_diffusion(C - 1, 1)
            dve.wait_ge(d_free, C + 1)

            def mask(n, par, waits):
                dve.wait_ge(q_ready, n + 1)
                if waits:
                    dve.wait_ge(y_used, n - 1)
                nc.vector.scalar_tensor_tensor(out=wt[:, par, :], in0=stage[:, par, :], scalar=col(C_E0),
                                               in1=adj8[:, n, :], op0=ALU.subtract, op1=ALU.mult).then_inc(y_ready, 1)

            def finish(c):
                dve.wait_ge(y_used, c * T + T)
                for k, n in BANKS:
                    ins = nc.vector.tensor_tensor(fin[:, k * BK:k * BK + n, :], accs(k, n),
                                                  tot[:, :].unsqueeze(1).broadcast_to([P, n, A]), ALU.add)
                ins.then_inc(acc_free, 1)
                dve.wait_ge(acc_free, C + 2 + c)
                nc.vector.reciprocal(rden[:, :], fin[:, :, D]).then_inc(fin_ready, 1)
                dve.wait_ge(fin_ready, 2 * c + 1)
                nc.vector.tensor_scalar(rden[:, :], rden[:, :], col(C_SIG), None, ALU.mult).then_inc(fin_ready, 1)
                dve.wait_ge(fin_ready, 2 * c + 2)
                for r in range(R):
                    row = res[:, bass.ds(c * R + r, 1), :].squeeze(1)
                    ins = nc.vector.scalar_tensor_tensor(out=row, in0=fin[:, r, 0:D], scalar=rden[:, r:r + 1],
                                                         in1=row, op0=ALU.mult, op1=ALU.add)
                ins.then_inc(out_ready, 1)

            def mask_rest(c):
                with dve.Fori(1, T // 2) as k:
                    mask(c * T + 2 * k, 0, True)
                    mask(c * T + 2 * k + 1, 1, True)

            mask(0, 0, False)
            mask(1, 1, False)
            with dve.Fori(0, C - 1) as c:
                mask_rest(c)
                mask(c * T + T, 0, True)
                mask(c * T + T + 1, 1, True)
                finish(c)
            mask_rest(C - 1)
            finish(C - 1)


def kernel(**inputs):
    import numpy as _np
    import concourse.bacc as _bacc
    from concourse import mybir as _mybir
    from concourse.bass_utils import run_bass_kernel_spmd as _run

    x = _np.ascontiguousarray(inputs["x"])
    n = x.shape[1]
    b = _np.asarray(inputs["L0_gnn_b"])
    W = _np.asarray(inputs["L0_gnn_W"])
    a_s = _np.asarray(inputs["L0_gnn_a_s"])
    arrays = {
        "x": x,
        "adjT": _np.asarray(inputs["adj"]).T,
        "W": W,
        "WT": W.T,
        "a_s_cols": _np.broadcast_to(a_s, (n, n)),
        "a_r": _np.asarray(inputs["L0_gnn_a_r"]),
        "a_s": a_s,
        "b_rows": _np.broadcast_to(b[None, :], (n, n)),
        "b_cols": _np.broadcast_to(b[:, None], (n, n)),
        "alpha": _np.broadcast_to(_np.asarray(inputs["L1_gnn_alpha"]), (n, 1)),
        "beta": _np.broadcast_to(_np.asarray(inputs["L1_gnn_beta"]), (n, 1)),
    }
    arrays = {k: _np.ascontiguousarray(v) for k, v in arrays.items()}
    nc = _bacc.Bacc("TRN2", target_bir_lowering=False, num_devices=1)
    args = [nc.dram_tensor(k, v.shape, _mybir.dt.from_np(v.dtype), kind="ExternalInput").ap()
            for k, v in arrays.items()]
    args.append(nc.dram_tensor("out", x.shape, _mybir.dt.from_np(x.dtype), kind="ExternalOutput").ap())
    gat_then_cosine_diffusion(nc, *args)
    r = _run(nc, [arrays], core_ids=[0])
    return r.results[0]["out"]
```

```python
from contextlib import ExitStack

import concourse.bass as bass
from concourse import mybir

ALU = mybir.AluOpType
ACT = mybir.ActivationFunctionType
F32 = mybir.dt.float32
F16 = mybir.dt.float16
BF16 = mybir.dt.bfloat16
U8 = mybir.dt.uint8
U16 = mybir.dt.uint16
AX = mybir.AxisListType

P = 128
SLOPE = 0.2
LN_EPS = 1e-5
COS_EPS = 1e-8
HN_SCALE = 256.0
DH_SCALE = 1024.0
H_SCALE = 64.0
EDGE = 4.0
Y_SCALE = 16.0


def gat_then_cosine_diffusion(nc, x, adjT, WT, params, out):
    N, D = x.shape
    T = N // P
    CW = 1024
    C = N // CW
    R = CW // P
    HW = CW // 2
    RH = R // 2
    A = D + 1
    BK = 3
    NT = C * T
    SLOTS = 4
    ASLOTS = 4
    TP = T // 2
    assert D == P and N == C * CW
    assert T * EDGE < 256

    def bank(r):
        return r // BK, (r % BK) * A

    BANKS = [(k, min(BK, R - BK * k)) for k in range((R + BK - 1) // BK)]

    def wait(engine, semaphore, value):
        if not (isinstance(value, int) and value <= 0):
            engine.wait_ge(semaphore, value)

    with ExitStack() as ctx:
        def sb(name, shape, dt=F32):
            return ctx.enter_context(nc.sbuf_tensor(name, shape, dt))

        def sem(name):
            return ctx.enter_context(nc.semaphore(name))

        adj8 = sb("adj8", [P, NT, CW], U8)
        stage = sb("stage", [P, SLOTS, CW])
        cbuf = sb("cbuf", [P, T * A])
        gbuf = sb("gbuf", [P, T, A])
        res = sb("res", [P, T, D])
        wt = sb("wt", [P, 2, CW])
        degs = sb("degs", [P, 2, HW], U16)
        degb = sb("degb", [P, CW], BF16)
        ident = sb("ident", [P, P])
        ones = sb("ones", [1, P])
        ones16 = sb("ones16", [P, P], F16)
        onesb = sb("onesb", [P, 2], BF16)
        hcol = sb("hcol", [P, R], F16)
        bst = sb("bst", [P, R, 6])
        mv = sb("mv", [P, 2, R, 2])
        pow_in = sb("pow_in", [P, 3, T])
        rstd = sb("rstd", [P, T])
        dis = sb("dis", [P, T])
        invn = sb("invn", [P, T])
        half = sb("half", [P, T])
        nmr = sb("nmr", [P, T])
        ssq = sb("ssq", [P, T])
        disd = sb("disd", [P, T])
        vj = sb("vj", [P, T])
        gj = sb("gj", [P, T])
        rden = sb("rden", [P, R])
        sc = sb("sc", [P, 16])

        (C_RMAX, C_RTOP, C_M8R, C_M2R, C_MBS, C_BAS, C_EMA, C_SIG, C_MSIG,
         C_BSC, C_NB, C_E0, C_AS, C_T) = range(14)

        def col(k):
            return sc[:, k:k + 1]

        def row(ap, t):
            return ap[:, bass.ds(t, 1), :].squeeze(1)

        def flat(ap):
            return ap.rearrange("p a b -> p (a b)")

        SHIFT = 16
        cb = cbuf[:, SHIFT:SHIFT + N]
        h1 = cbuf[:, SHIFT:SHIFT + N].rearrange("p (t d) -> p t d", d=D)
        hp = cbuf[:, :].bitcast(F16)[:, 0:T * (2 * D + 1)].rearrange("p (t a) -> p t a", a=2 * D + 1)
        late = flat(adj8[:, NT - T:NT, :]).bitcast(F32)
        h0T = late[:, 0:T * D]
        h0 = late[:, T * D:2 * T * D].rearrange("p (t d) -> p t d", d=D)
        wt3 = flat(adj8[:, NT - 4:NT, :]).bitcast(F32)
        wk = flat(adj8[:, NT - T - 4:NT - T, :]).bitcast(F32)
        par_sb = wk[:, 0:4 * P + 4]
        w_sb, as_sb, bc_sb = wk[:, 0:P], wk[:, P:2 * P], wk[:, 2 * P:3 * P]
        ar_as = wk[:, 3 * P:3 * P + 2]
        alpha, beta = wk[:, 3 * P + 2:3 * P + 3], wk[:, 3 * P + 3:3 * P + 4]
        brow = wk[:, 3 * P + 4:4 * P + 5]
        wtr = wk[:, 4 * P + 8:4 * P + 8 + A]
        ws_sb = wk[:, 6 * P:7 * P]
        adj_pairs = flat(adj8[:, :, :]).bitcast(U16).rearrange("p (n i) -> p n i", i=HW)
        dh = flat(stage[:, :, :]).bitcast(F16).rearrange("p (t k d) -> p t k d", k=2, d=D)
        yp = flat(stage[:, 0:2, :]).bitcast(F16).rearrange("p (b k i) -> p b k i", b=2, k=2)
        fin = flat(stage[:, 2:4, :])[:, 0:R * A].rearrange("p (r a) -> p r a", a=A)
        hnT = flat(gbuf[:, :, :])[:, 0:N].bitcast(F16).rearrange("p (k i) -> p k i", k=2)
        hn = flat(degs[:, :, :]).bitcast(F32).rearrange("p (t d) -> p t d", d=D)
        tot = degb[:, :].bitcast(F32)[:, 0:A]
        a16 = wt[:, 0, :].bitcast(BF16).rearrange("p (s i) -> p s i", s=ASLOTS)
        hparts = wt[:, 1, :].bitcast(F16).rearrange("p (k t d) -> p k t d", k=2, d=D)

        ps = ctx.enter_context(nc.psum_tensor("ps", [P, 8, 512], F32))

        def area(k):
            return flat(ps[:, 2 * k:2 * k + 2, :])

        def first_bank(c):
            return 4 * (c % 2)

        def acc(fb, r, width):
            b, o = bank(r)
            return ps[:, fb + b, o:o + width]

        def accs(fb, k, n):
            return ps[:, fb + k, 0:n * A].rearrange("p (r a) -> p r a", a=A)

        def buffers(c):
            return 3 if c < C - 1 else 2

        def weights(n, c):
            b = n % buffers(c)
            return wt3 if b == 2 else wt[:, b, :]

        x_loaded = [sem(f"x_loaded{q}") for q in range(C)]
        w_loaded = sem("w_loaded")
        stage_loaded = [sem(f"stage_loaded{s}") for s in range(SLOTS)]
        adj_kept = sem("adj_kept")
        consts_ready = sem("consts_ready")
        pow_asked = sem("pow_asked")
        pow_done = sem("pow_done")
        dve_step = sem("dve_step")
        wprod_ready = sem("wprod_ready")
        wprod_kept = sem("wprod_kept")
        nmr_ready = sem("nmr_ready")
        h0_ready = [sem(f"h0_ready{q}") for q in range(C)]
        h0T_psum = sem("h0T_psum")
        h0T_ready = sem("h0T_ready")
        H_psum = sem("H_psum")
        H_kept = sem("H_kept")
        s_psum = sem("s_psum")
        rmax_part = sem("rmax_part")
        rmax_row = sem("rmax_row")
        rmax_one = sem("rmax_one")
        rmax_all = sem("rmax_all")
        shift_ready = sem("shift_ready")
        vg_ready = sem("vg_ready")
        c_raw = sem("c_raw")
        scal_ready = sem("scal_ready")
        g_ready = sem("g_ready")
        c_ready = sem("c_ready")
        p_ready = sem("p_ready")
        p_used = sem("p_used")
        count_step = sem("count_step")
        degb_ready = sem("degb_ready")
        deg_psum = sem("deg_psum")
        acc_free = sem("acc_free")
        h1_ready = sem("h1_ready")
        ssq_ready = sem("ssq_ready")
        dh_hi = sem("dh_hi")
        dh_lo = sem("dh_lo")
        a16_dve = sem("a16_dve")
        a16_act = sem("a16_act")
        a16_used = sem("a16_used")
        d_free = [sem(f"d_free{k}") for k in range(2)]
        d_step = sem("d_step")
        hn_ready = sem("hn_ready")
        hnT_psum = sem("hnT_psum")
        hnT_hi = sem("hnT_hi")
        hnT_lo = sem("hnT_lo")
        hp_hi = sem("hp_hi")
        hp_ready = sem("hp_ready")
        tot_psum = sem("tot_psum")
        z_ready = sem("z_ready")
        q_ready = sem("q_ready")
        y_ready = sem("y_ready")
        yhi_ready = sem("yhi_ready")
        ylo_ready = sem("ylo_ready")
        y_used = sem("y_used")
        fin_step = sem("fin_step")
        out_ready = sem("out_ready")
        stored = sem("stored")

        xt = x.rearrange("(t p) d -> p t d", p=P)
        ot = out.rearrange("(t p) d -> p t d", p=P)
        at = adjT.rearrange("(t p) (c i) -> c t p i", p=P, i=CW)

        POW_LN0 = [q + 1 for q in range(C)]

        def POW_DIS(c):
            return C + 2 * c + 1

        def POW_LN1(c):
            return C + 2 * c + 2

        POW_NORM = 3 * C + 1

        block = ctx.enter_context(nc.Block())

        @block.sync
        def _(sp):
            sp.dma_start(par_sb, params).then_inc(w_loaded, 16)
            sp.dma_start(wtr[:, 0:D], WT).then_inc(w_loaded, 16)
            for q in range(C):
                sp.dma_start(res[:, q * R:(q + 1) * R, :], xt[:, q * R:(q + 1) * R, :]).then_inc(x_loaded[q], 16)

            def load(c, g, first):
                for s in range(SLOTS):
                    if not first:
                        sp.wait_ge(adj_kept, c * T + g * SLOTS + s - (SLOTS - 1))
                    sp.dma_start(stage[:, s, :], at[c, g * SLOTS + s]).then_inc(stage_loaded[s], 16)

            load(0, 0, True)
            with sp.Fori(1, T // SLOTS) as g:
                load(0, g, False)
            with sp.Fori(1, C) as c:
                with sp.Fori(0, T // SLOTS) as g:
                    load(c, g, False)
            for c in range(C):
                sp.wait_ge(out_ready, c + 1)
                sp.dma_start(ot[:, c * R:(c + 1) * R, :], res[:, c * R:(c + 1) * R, :]).then_inc(stored, 16)
            sp.wait_ge(stored, 16 * C)

        @block.gpsimd
        def _(pool):
            pool.memset(ident[:, :], 0.0).then_inc(consts_ready, 1)
            pool.memset(half[:, :], -0.5).then_inc(consts_ready, 1)
            pool.memset(ones[:, :], 1.0).then_inc(consts_ready, 1)
            pool.memset(ones16[:, :], 1.0).then_inc(consts_ready, 1)
            pool.memset(onesb[:, :], 1.0).then_inc(consts_ready, 1)
            pool.memset(hcol[:, :], H_SCALE).then_inc(consts_ready, 1)
            pool.wait_ge(consts_ready, 6)
            pool.affine_select(out=ident[:, :], in_=ident[:, :], compare_op=ALU.not_equal, fill=1.0, base=0,
                               pattern=[[-1, P]], channel_multiplier=1).then_inc(consts_ready, 1)
            chunk_cols = [slice(q * R, (q + 1) * R) for q in range(C)]
            asks = [(rstd, 0, w) for w in chunk_cols]
            for w in chunk_cols:
                asks += [(dis, 1, w), (rstd, 0, w)]
            asks.append((invn, 2, slice(0, T)))
            for k, (dst, src, w) in enumerate(asks):
                pool.wait_ge(pow_asked, k + 1)
                nc.gpsimd.tensor_tensor(dst[:, w], pow_in[:, src, w], half[:, w], ALU.pow).then_inc(pow_done, 1)

        @block.scalar
        def _(act):
            def normalize(dst, t):
                return nc.scalar.activation(dst, res[:, t, :], ACT.Relu, bias=nmr[:, t:t + 1], scale=rstd[:, t:t + 1])

            act.wait_ge(wprod_ready, 1)
            nc.scalar.activation(wtr[:, D:A], ps[:, 7, 128:129], ACT.Copy).then_inc(wprod_kept, 1)
            nc.scalar.activation(brow[:, D:A], ps[:, 7, 130:131], ACT.Copy).then_inc(wprod_kept, 1)
            nc.scalar.activation(col(C_BAS), ps[:, 7, 131:132], ACT.Copy).then_inc(wprod_kept, 1)
            nc.scalar.activation(ws_sb, ps[:, 7, 0:P], ACT.Copy).then_inc(wprod_kept, 1)
            nc.scalar.activation(col(C_EMA), alpha, ACT.Exp, scale=-1.0).then_inc(scal_ready, 1)
            for q in range(C):
                act.wait_ge(h0T_psum, q + 1)
                nc.scalar.activation(h0T[:, q * CW:(q + 1) * CW], area(q % 2), ACT.Copy).then_inc(h0T_ready, 1)
                if q == 0:
                    act.wait_ge(nmr_ready, 1)
                    for t in range(R, 2 * R):
                        ins = normalize(h0[:, t, :], t)
                    ins.then_inc(h0_ready[1], 1)

            def keep(g):
                for s in range(SLOTS):
                    act.wait_ge(stage_loaded[s], 16 * g + 16)
                    nc.scalar.activation(adj8[:, g * SLOTS + s, :], stage[:, s, :], ACT.Copy,
                                         scale=EDGE).then_inc(adj_kept, 1)

            keep(0)
            act.wait_ge(shift_ready, 1)
            nc.scalar.activation(gj[:, :], gbuf[:, :, D], ACT.Exp, bias=col(C_M2R), scale=SLOPE).then_inc(vg_ready, 1)
            nc.scalar.activation(vj[:, :], gbuf[:, :, D], ACT.Exp, bias=col(C_M8R), scale=1 - SLOPE).then_inc(vg_ready, 1)

            def c_exp(q):
                act.wait_ge(s_psum, q + 1)
                nc.scalar.activation(cb[:, q * CW:(q + 1) * CW], area(0 if q == 0 else 2), ACT.Exp, bias=col(C_MBS),
                                     scale=-(1 - SLOPE)).then_inc(c_raw, 1)

            GC = T // SLOTS
            c_exp(0)
            nc.scalar.activation(col(C_E0), col(C_NB), ACT.Exp).then_inc(scal_ready, 1)
            for q in range(1, C):
                with act.Fori((1, 2, 6)[q - 1], (2, 6, 9)[q - 1]) as g:
                    keep(g)
                c_exp(q)

            def norm1(c):
                act.wait_ge(nmr_ready, 2 + c)
                for t in range(c * R, (c + 1) * R):
                    ins = normalize(h1[:, t, :], t)
                ins.then_inc(h1_ready, 1)

            AHEAD = 5
            with act.Fori(9, GC + AHEAD) as g:
                keep(g)
            act.wait_ge(g_ready, C)
            for c in range(C - 1):
                norm1(c)
                with act.Fori((c + 1) * GC + AHEAD, min((c + 2) * GC + AHEAD, C * GC)) as g:
                    keep(g)

            def dis_h(q):
                act.wait_ge(pow_done, POW_DIS(q))
                for t in range(q * R, (q + 1) * R):
                    ins = nc.scalar.activation(dh[:, t, 0, :], h1[:, t, :], ACT.Copy, scale=dis[:, t:t + 1])
                ins.then_inc(dh_hi, 1)

            def squares(q):
                act.wait_ge(h1_ready, q + 1)
                if q >= 1:
                    act.wait_ge(ssq_ready, q)
                for t in range(R):
                    ins = nc.scalar.activation(area(1)[:, t * D:(t + 1) * D], h1[:, q * R + t, :], ACT.Square,
                                               accum_out=ssq[:, q * R + t:q * R + t + 1])
                ins.then_inc(ssq_ready, 1)

            act.wait_ge(adj_kept, NT)
            for q in range(C - 1):
                dis_h(q)
            act.wait_ge(acc_free, C - 1)
            for q in range(C - 1):
                squares(q)

            def widen(c, hf, g):
                for s in range(ASLOTS // 2, ASLOTS):
                    k = (2 * c + hf) * T + g * ASLOTS + s
                    wait(act, a16_used, k - (ASLOTS - 1))
                    nc.scalar.activation(a16[:, s, :], adj8[:, c * T + g * ASLOTS + s, hf * HW:(hf + 1) * HW],
                                         ACT.Copy).then_inc(a16_act, 1)

            def make_hn(c, hf):
                for t in range(RH):
                    tile = c * R + hf * RH + t
                    ins = nc.scalar.activation(hn[:, t, :], row(h1, tile), ACT.Copy, scale=invn[:, bass.ds(tile, 1)])
                ins.then_inc(hn_ready, 1)

            def hnT_high(sub, hf):
                act.wait_ge(hnT_psum, sub)
                w = bass.ds((sub - 1) * HW, HW)
                nc.scalar.activation(hnT[:, 0, w], ps[:, 4 + hf, :], ACT.Copy).then_inc(hnT_hi, 1)

            def beside_diffusion(c, hf):
                sub = 2 * c + hf
                first = isinstance(c, int) and sub == 0
                widen(c, hf, 0)
                if first:
                    widen(c, hf, 1)
                    norm1(C - 1)
                    act.wait_ge(h1_ready, C)
                    dis_h(C - 1)
                    squares(C - 1)
                else:
                    hnT_high(sub, 1 - hf)
                    widen(c, hf, 1)
                    make_hn(c, hf)
                if hf == 1:
                    nc.scalar.activation(hparts[:, 0, :, :], h1[:, bass.ds(c * R, R), :], ACT.Copy,
                                         scale=H_SCALE).then_inc(hp_hi, 1)
                for g in range(2, GC):
                    widen(c, hf, g)
                    if first and g == 5:
                        act.wait_ge(pow_done, POW_NORM)
                        act.wait_ge(degb_ready, C)
                        make_hn(c, hf)

            act.wait_ge(p_used, NT)
            beside_diffusion(0, 0)
            beside_diffusion(0, 1)
            with act.Fori(1, C) as c:
                beside_diffusion(c, 0)
                beside_diffusion(c, 1)
            hnT_high(2 * C, 1)

            def expo(n, par):
                act.wait_ge(z_ready, n + 1)
                nc.scalar.activation(area(par), area(par), ACT.Exp, bias=col(C_NB),
                                     scale=col(C_BSC)).then_inc(q_ready, 1)

            def y_high(n, par):
                act.wait_ge(y_ready, n + 1)
                wait(act, y_used, n - 1)
                nc.scalar.activation(yp[:, par, 0, :], wt[:, par, :], ACT.Copy,
                                     scale=Y_SCALE).then_inc(yhi_ready, 1)

            act.wait_ge(a16_used, 2 * NT)
            expo(0, 0)
            expo(1, 1)
            y_high(0, 0)
            expo(2, 0)
            y_high(1, 1)
            with act.Fori(1, NT // 2 - 1) as k:
                expo(2 * k + 1, 1)
                y_high(2 * k, 0)
                expo(2 * k + 2, 0)
                y_high(2 * k + 1, 1)
            expo(NT - 1, 1)
            y_high(NT - 2, 0)
            y_high(NT - 1, 1)

        @block.tensor
        def _(pe):
            pe.wait_ge(w_loaded, 16 * 2)
            pe.matmul(ps[:, 7, 0:P], w_sb, as_sb, start=True, stop=True)
            pe.matmul(ps[:, 7, 128:129], w_sb, ar_as[:, 0:1], start=True, stop=True)
            pe.matmul(ps[:, 7, 130:132], bc_sb, ar_as, start=True, stop=True).then_inc(wprod_ready, 1)
            pe.wait_ge(consts_ready, 7)

            def turn_h0(q):
                pe.wait_ge(h0_ready[q], 1)
                if q >= 2:
                    pe.wait_ge(h0T_ready, q - 1)
                for t in range(R):
                    mm = pe.transpose(area(q % 2)[:, t * P:(t + 1) * P], h0[:, q * R + t, :], ident[:, :])
                mm.then_inc(h0T_psum, 1)

            def project(q):
                pe.wait_ge(h0T_ready, q + 1)
                if q == 0:
                    pe.wait_ge(wprod_kept, 4)
                if q >= 1:
                    pe.wait_ge(H_kept, q)
                for t in range(R):
                    mm = pe.matmul(acc(4, t, A), h0T[:, (q * R + t) * P:(q * R + t + 1) * P], wtr,
                                   start=True, stop=True)
                mm.then_inc(H_psum, 1)

            def scores(q):
                for f in range(CW // 512):
                    mm = pe.matmul(ps[:, (0 if q == 0 else 4) + f, :], ws_sb,
                                   h0T[:, q * CW + f * 512:q * CW + (f + 1) * 512], start=True, stop=True)
                mm.then_inc(s_psum, 1)

            turn_h0(0)
            project(0)
            turn_h0(1)
            turn_h0(2)
            project(1)
            turn_h0(3)
            project(2)
            pe.wait_ge(h0T_ready, C)
            scores(0)
            project(3)
            pe.wait_ge(rmax_part, 1)
            pe.transpose(ps[0:1, 7, 256:256 + P], col(C_RMAX), ident[:, :]).then_inc(rmax_row, 1)
            pe.wait_ge(rmax_one, 1)
            pe.matmul(ps[:, 7, 400:401], ones[:, :], sc[0:1, C_RTOP:C_RTOP + 1],
                      start=True, stop=True).then_inc(rmax_all, 1)

            def attend(c, k, k0=0):
                fb = first_bank(c)
                for t in (2 * k, 2 * k + 1):
                    n = c * T + t
                    pe.wait_ge(p_ready, 2 * k0 + n + 1)
                    for r in range(R):
                        mm = pe.matmul(acc(fb, r, A), weights(n, c)[:, r * P:(r + 1) * P], row(gbuf, 2 * k0 + t),
                                       start=t == 0 and isinstance(k0, int) and r % BK == 0, stop=False,
                                       skip_group_check=True)
                    mm.then_inc(p_used, 1)

            def attend_three(c, k, k0=0):
                for m in range(k, k + 3):
                    attend(c, m, k0)

            def degrees(c):
                pe.wait_ge(degb_ready, c + 1)
                for r in range(R):
                    mm = pe.matmul(ps[:, first_bank(c) + 3, r:r + 1], degb[:, r * P:(r + 1) * P], onesb[:, 0:1],
                                   start=r == 0, stop=r == R - 1, skip_group_check=True)
                mm.then_inc(deg_psum, 1)

            for c in range(C):
                if c == 0:
                    attend(0, 0)
                    scores(1)
                    for q in range(1, C):
                        pe.wait_ge(g_ready, q + 1)
                        attend(c, q)
                    for q in range(2, C):
                        attend_three(0, C + 3 * (q - 2))
                        pe.wait_ge(c_raw, q)
                        scores(q)
                    done = C + 3 * (C - 2)
                else:
                    if c == 1:
                        pe.wait_ge(c_raw, C)
                    else:
                        pe.wait_ge(acc_free, c - 1)
                    for k in range(4):
                        attend(c, k)
                        if k == 1:
                            degrees(c - 1)
                    done = 4
                with pe.Fori(0, (TP - done) // 3) as kk:
                    attend_three(c, done, 3 * kk)
            degrees(C - 1)

            def diffuse(c, hf, t):
                k = (2 * c + hf) * (T // 2) + (t // ASLOTS) * (ASLOTS // 2) + t % (ASLOTS // 2) + 1
                pe.wait_ge(a16_dve if t % ASLOTS < ASLOTS // 2 else a16_act, k)
                if t % R == 0:
                    pe.wait_ge(dh_lo, t // R + 1)
                for r in range(RH):
                    mm = pe.matmul(ps[:, 2 * hf + r // 2, (r % 2) * 2 * D:(r % 2 + 1) * 2 * D],
                                   a16[:, t % ASLOTS, r * P:(r + 1) * P], dh[:, t, :, :].rearrange("p k d -> p (k d)"),
                                   start=t == 0 and r % 2 == 0, stop=t == T - 1, skip_group_check=True)
                mm.then_inc(a16_used, 1)

            def diffuse_half(c, hf):
                pe.wait_ge(d_free[hf], c + 1)
                for t in range(T - ASLOTS):
                    diffuse(c, hf, t)
                pe.wait_ge(hn_ready, 2 * c + hf + 1)
                for t in range(RH):
                    mm = pe.transpose(ps[:, 4 + hf, t * P:(t + 1) * P], hn[:, t, :], ident[:, :])
                mm.then_inc(hnT_psum, 1)
                for t in range(T - ASLOTS, T):
                    diffuse(c, hf, t)

            with pe.Fori(0, C) as c:
                diffuse_half(c, 0)
                pe.wait_ge(ssq_ready, C)
                diffuse_half(c, 1)

            def cosine(c, t, n, par):
                wait(pe, y_ready, n - 1)
                if isinstance(n, int) and n < 2:
                    pe.wait_ge(d_free[par], C + 1)
                for a, b in ((0, 0), (0, 1), (1, 0)):
                    for f in range(CW // 512):
                        mm = pe.matmul(ps[:, 2 * par + f, :], hnT[:, a, bass.ds(t * P, P)],
                                       hnT[:, b, bass.ds(c * CW + f * 512, 512)],
                                       start=(a, b) == (0, 0), stop=a == 1, skip_group_check=True)
                mm.then_inc(z_ready, 1)

            def weigh(t, n, par, first=False):
                pe.wait_ge(ylo_ready, n + 1)
                for r in range(R):
                    hi, lo = (yp[:, par, k, r * P:(r + 1) * P] for k in range(2))
                    pe.matmul(acc(4, r, A), hi, hp[:, t, 0:A], start=first and r % BK == 0, stop=False,
                              skip_group_check=True)
                    pe.matmul(acc(4, r, D), hi, hp[:, t, A:A + D], start=False, stop=False, skip_group_check=True)
                    mm = pe.matmul(acc(4, r, A), lo, hp[:, t, 0:A], start=False, stop=False, skip_group_check=True)
                mm.then_inc(y_used, 1)

            cosine(0, 0, 0, 0)
            cosine(0, 1, 1, 1)
            pe.wait_ge(hnT_lo, 2 * C)
            pe.wait_ge(hp_ready, C)
            for t in range(T):
                pe.matmul(ps[:, 7, 0:A], ones16[:, :], hp[:, t, 0:A], start=(t == 0), stop=False, skip_group_check=True)
                mm = pe.matmul(ps[:, 7, 0:D], ones16[:, :], hp[:, t, A:A + D], start=False, stop=(t == T - 1),
                               skip_group_check=True)
            mm.then_inc(tot_psum, 1)
            cosine(0, 2, 2, 0)
            AHEAD = 3
            for c in range(C):
                for t in range(4):
                    n = c * T + t
                    cosine(c, t + AHEAD, n + AHEAD, (t + AHEAD) % 2)
                    if t == 0 and c >= 1:
                        pe.wait_ge(acc_free, C + c)
                    weigh(t, n, t % 2, t == 0)
                with pe.Fori(1, T // 4 - 1) as g:
                    for s in range(4):
                        cosine(c, 4 * g + s + AHEAD, c * T + 4 * g + s + AHEAD, (s + AHEAD) % 2)
                        weigh(4 * g + s, c * T + 4 * g + s, s % 2)
                for t in range(T - 4, T):
                    n = c * T + t
                    if t + AHEAD < T:
                        cosine(c, t + AHEAD, n + AHEAD, (t + AHEAD) % 2)
                    elif c + 1 < C:
                        cosine(c + 1, t + AHEAD - T, n + AHEAD, (t + AHEAD) % 2)
                    weigh(t, n, t % 2)

        @block.vector
        def _(dve):
            class Chain:
                def __init__(self, semaphore, base=0):
                    self.semaphore, self.base, self.k = semaphore, base, 0

                def link(self, ins):
                    self.k += 1
                    ins.then_inc(self.semaphore, 1)
                    dve.wait_ge(self.semaphore, self.base + self.k)

            pro = Chain(dve_step)

            def row_stats(c, rows):
                for t in rows:
                    ins = nc.vector.bn_stats(bst[:, t, :], res[:, c * R + t, :])
                pro.link(ins)

            def ask_rstd(c, m=0):
                for t in range(R):
                    ins = nc.vector.bn_aggr(mv[:, m, t, :], bst[:, t, :])
                pro.link(ins)
                nc.vector.tensor_scalar(pow_in[:, 0, c * R:(c + 1) * R], mv[:, m, :, 1], LN_EPS, None,
                                        ALU.add).then_inc(pow_asked, 1)

            def statistics(c, m=0):
                row_stats(c, range(R))
                ask_rstd(c, m)

            def mean_shift(c, answer, m=0):
                dve.wait_ge(pow_done, answer)
                w = slice(c * R, (c + 1) * R)
                nc.vector.scalar_tensor_tensor(out=nmr[:, w], in0=mv[:, m, :, 0], scalar=-1.0, in1=rstd[:, w],
                                               op0=ALU.mult, op1=ALU.mult).then_inc(nmr_ready, 1)

            def center(q, m):
                w = slice(q * R, (q + 1) * R)
                pro.link(nc.vector.tensor_tensor(h0[:, w, :], res[:, w, :],
                                                 mv[:, m, :, 0:1].broadcast_to([P, R, D]), ALU.subtract))

            def norm0(q):
                dve.wait_ge(pow_done, POW_LN0[q])
                w = slice(q * R, (q + 1) * R)
                nc.vector.scalar_tensor_tensor(
                    out=h0[:, w, :], in0=h0[:, w, :], scalar=0.0, in1=rstd[:, w].unsqueeze(2).broadcast_to([P, R, D]),
                    op0=ALU.max, op1=ALU.mult).then_inc(h0_ready[q], 1)

            def keep_H(q):
                dve.wait_ge(H_psum, q + 1)
                for k, n in BANKS:
                    t0 = q * R + k * BK
                    ins = nc.vector.tensor_tensor(gbuf[:, t0:t0 + n, :], accs(4, k, n),
                                                  brow.unsqueeze(1).broadcast_to([P, n, A]), ALU.add)
                ins.then_inc(H_kept, 1)

            dve.wait_ge(x_loaded[0], 16)
            statistics(0, 0)
            dve.wait_ge(x_loaded[1], 16)
            statistics(1, 1)
            center(0, 0)
            norm0(0)
            mean_shift(1, POW_LN0[1], 1)
            dve.wait_ge(x_loaded[2], 16)
            statistics(2, 0)
            dve.wait_ge(x_loaded[3], 16)
            statistics(3, 1)
            center(2, 0)
            norm0(2)
            center(3, 1)
            norm0(3)
            dve.wait_ge(scal_ready, 1)
            pro.link(nc.vector.tensor_scalar(col(C_T), col(C_EMA), 1.0, None, ALU.add))
            pro.link(nc.vector.reciprocal(col(C_SIG), col(C_T)))
            nc.vector.tensor_scalar(col(C_MSIG), col(C_SIG), -1.0, -1.0, ALU.mult, ALU.add)
            nc.vector.tensor_scalar(col(C_BSC), beta, 1.0 / HN_SCALE ** 2, None, ALU.mult)
            nc.vector.scalar_tensor_tensor(out=col(C_NB), in0=beta, scalar=-1.0, in1=beta, op0=ALU.mult, op1=ALU.min)
            dve.wait_ge(wprod_kept, 4)
            pro.link(nc.vector.tensor_scalar(col(C_AS), col(C_BAS), -(1 - SLOPE), None, ALU.mult))
            for q in range(C):
                keep_H(q)
            dve.wait_ge(H_kept, C)
            nc.vector.tensor_reduce(col(C_RMAX), gbuf[:, :, D], AX.X, ALU.max).then_inc(rmax_part, 1)
            dve.wait_ge(rmax_row, 1)
            nc.vector.tensor_reduce(sc[0:1, C_RTOP:C_RTOP + 1], ps[0:1, 7, 256:256 + P], AX.X,
                                    ALU.max).then_inc(rmax_one, 1)
            dve.wait_ge(rmax_all, 1)
            nc.vector.tensor_scalar(col(C_M2R), ps[:, 7, 400:401], -SLOPE, None, ALU.mult)
            pro.link(nc.vector.tensor_scalar(col(C_M8R), ps[:, 7, 400:401], -(1 - SLOPE), None, ALU.mult))
            nc.vector.tensor_tensor(col(C_MBS), col(C_AS), col(C_M8R), ALU.add).then_inc(shift_ready, 1)

            def scale_H(q):
                w = slice(q * R, (q + 1) * R)
                nc.vector.tensor_tensor(gbuf[:, w, 0:D], gbuf[:, w, 0:D],
                                        gj[:, w].unsqueeze(2).broadcast_to([P, R, D]), ALU.mult)
                nc.vector.tensor_copy(gbuf[:, w, D], gj[:, w]).then_inc(g_ready, 1)

            def cap_c(q):
                dve.wait_ge(c_raw, q + 1)
                w = slice(q * CW, (q + 1) * CW)
                nc.vector.tensor_scalar(cb[:, w], cb[:, w], 1.0, None, ALU.min).then_inc(c_ready, 1)

            def edge_weights(c, t, t0=0):
                n = c * T + t
                dve.wait_ge(adj_kept, t0 + n + 1)
                wait(dve, p_used, t0 + n + 1 - buffers(c))
                nc.vector.scalar_tensor_tensor(out=weights(n, c), in0=cb[:, c * CW:(c + 1) * CW],
                                               scalar=vj[:, bass.ds(t0 + t, 1)], in1=row(adj8, t0 + n),
                                               op0=ALU.max, op1=ALU.mult).then_inc(p_ready, 1)

            def count_edges(c, k, k0=0):
                m = k0 + c * TP + k
                if isinstance(k0, int) and k == 0:
                    return
                if isinstance(k0, int) and k == 1:
                    wait(dve, degb_ready, c)
                    before = adj_pairs[:, 2 * m - 2:2 * m, :]
                else:
                    dve.wait_ge(count_step, m - 1)
                    before = degs[:, :, :]
                nc.vector.tensor_tensor(degs[:, :, :], before, adj_pairs[:, bass.ds(2 * m, 2), :],
                                        ALU.add).then_inc(count_step, 1)

            def sum_counts(c):
                dve.wait_ge(count_step, (c + 1) * TP - 1)
                wait(dve, deg_psum, c)
                even, odd = (degs[:, k, :].bitcast(U8) for k in range(2))
                nc.vector.tensor_tensor(degb[:, :], even, odd, ALU.add).then_inc(degb_ready, 1)
                dve.sem_inc(count_step, 1)

            def edge_pair(c, k, k0=0):
                edge_weights(c, 2 * k, 2 * k0)
                edge_weights(c, 2 * k + 1, 2 * k0)
                count_edges(c, k, k0)

            def edge_pairs(c, done):
                with dve.Fori(0, (TP - done) // 3) as kk:
                    for k in range(done, done + 3):
                        edge_pair(c, k, 3 * kk)

            def ask_dis(c):
                dve.wait_ge(deg_psum, c + 1)
                nc.vector.tensor_scalar(pow_in[:, 1, c * R:(c + 1) * R], ps[:, first_bank(c) + 3, 0:R], EDGE,
                                        1.0 / (EDGE * DH_SCALE ** 2), ALU.max, ALU.mult).then_inc(pow_asked, 1)

            def invert_den(c):
                dve.wait_ge(p_used, (c + 1) * T)
                for k, n in BANKS:
                    ins = nc.vector.reciprocal(rden[:, k * BK:k * BK + n], accs(first_bank(c), k, n)[:, :, D])
                pro.link(ins)

            def add_attention(c, rows):
                for r in rows:
                    dst = res[:, c * R + r, :]
                    ins = nc.vector.scalar_tensor_tensor(out=dst, in0=acc(first_bank(c), r, D), scalar=rden[:, r:r + 1],
                                                         in1=dst, op0=ALU.mult, op1=ALU.add)
                if R - 1 in rows:
                    ins.then_inc(acc_free, 1)

            low, high = range(R // 2), range(R // 2, R)
            dve.wait_ge(vg_ready, 2)
            scale_H(0)
            cap_c(0)
            dve.wait_ge(c_ready, 1)
            edge_weights(0, 0)
            edge_weights(0, 1)
            scale_H(1)
            scale_H(2)
            edge_pair(0, 1)
            scale_H(3)
            edge_pair(0, 2)
            edge_pair(0, 3)
            edge_pairs(0, 4)
            cap_c(1)
            for c in range(1, C):
                dve.wait_ge(c_ready, c + 1)
                edge_weights(c, 0)
                sum_counts(c - 1)
                edge_weights(c, 1)
                edge_pair(c, 1)
                invert_den(c - 1)
                add_attention(c - 1, low)
                edge_pair(c, 2)
                add_attention(c - 1, high)
                edge_pair(c, 3)
                ask_dis(c - 1)
                dve.wait_ge(acc_free, c)
                row_stats(c - 1, low)
                edge_pair(c, 4)
                row_stats(c - 1, high)
                edge_pair(c, 5)
                ask_rstd(c - 1)
                edge_pair(c, 6)
                mean_shift(c - 1, POW_LN1(c - 1))
                if c + 1 < C:
                    cap_c(c + 1)
                edge_pairs(c, 7)
            sum_counts(C - 1)

            def dis_h_low(q):
                dve.wait_ge(dh_hi, q + 1)
                for t in range(q * R, (q + 1) * R):
                    ins = nc.vector.scalar_tensor_tensor(out=dh[:, t, 1, :], in0=h1[:, t, :], scalar=dis[:, t:t + 1],
                                                         in1=dh[:, t, 0, :], op0=ALU.mult, op1=ALU.subtract)
                ins.then_inc(dh_lo, 1)

            def widen(c, hf, g):
                for s in range(ASLOTS // 2):
                    k = (2 * c + hf) * T + g * ASLOTS + s
                    wait(dve, a16_used, k - (ASLOTS - 1))
                    nc.vector.tensor_copy(a16[:, s, :],
                                          adj8[:, c * T + g * ASLOTS + s, hf * HW:(hf + 1) * HW]).then_inc(a16_dve, 1)

            def take_diffusion(chain, c, hf, part):
                dve.wait_ge(a16_used, (2 * c + hf + 1) * T)
                for r in range(RH):
                    tile = c * R + hf * RH + r
                    o = (r % 2) * 2 * D + part * D
                    ins = nc.vector.scalar_tensor_tensor(
                        out=row(res, tile), in0=ps[:, 2 * hf + r // 2, o:o + D], scalar=disd[:, bass.ds(tile, 1)],
                        in1=row(res, tile), op0=ALU.mult, op1=ALU.add)
                if part:
                    chain.link(ins)
                else:
                    ins.then_inc(d_free[hf], 1)

            def hnT_low(sub, hf):
                dve.wait_ge(hnT_hi, sub)
                w = bass.ds((sub - 1) * HW, HW)
                nc.vector.tensor_tensor(hnT[:, 1, w], ps[:, 4 + hf, :], hnT[:, 0, w], ALU.subtract).then_inc(hnT_lo, 1)

            def drop_h1(chain, c):
                w = bass.ds(c * R, R)
                chain.link(nc.vector.scalar_tensor_tensor(out=res[:, w, :], in0=h1[:, w, :], scalar=col(C_MSIG),
                                                          in1=res[:, w, :], op0=ALU.mult, op1=ALU.add))

            def split_h1(chain, c):
                w = bass.ds(c * R, R)
                dve.wait_ge(hp_hi, c + 1)
                chain.link(nc.vector.scalar_tensor_tensor(out=hparts[:, 1, :, :], in0=h1[:, w, :], scalar=H_SCALE,
                                                          in1=hparts[:, 0, :, :], op0=ALU.mult, op1=ALU.subtract))

            def place_hp(c):
                w = bass.ds(c * R, R)
                nc.vector.tensor_copy(hp[:, w, D], hcol[:, :])
                nc.vector.tensor_copy(hp[:, w, 0:D], hparts[:, 0, :, :])
                nc.vector.tensor_copy(hp[:, w, A:A + D], hparts[:, 1, :, :]).then_inc(hp_ready, 1)

            def beside_diffusion(chain, c, hf):
                sub = 2 * c + hf
                for g in range(T // ASLOTS):
                    widen(c, hf, g)
                    if g == 1:
                        hnT_low(sub, 1 - hf)
                        take_diffusion(chain, c - 1 + hf, 1 - hf, 1)
                    if g == 2:
                        take_diffusion(chain, c - 1 + hf, 1 - hf, 0)
                    if g == 3 and hf == 0:
                        drop_h1(chain, c)
                    if g == 3 and hf == 1:
                        split_h1(chain, c)
                    if g == 4 and hf == 1:
                        place_hp(c)

            nc.vector.tensor_scalar(disd[:, 0:TP], dis[:, 0:TP], 1.0 / (EDGE * DH_SCALE ** 2), None,
                                    ALU.mult).then_inc(d_free[0], 1)
            dis_h_low(0)
            dve.wait_ge(p_used, NT)
            widen(0, 0, 0)
            ask_dis(C - 1)
            invert_den(C - 1)
            add_attention(C - 1, range(R))
            dve.wait_ge(acc_free, C)
            statistics(C - 1)
            dis_h_low(1)
            mean_shift(C - 1, POW_LN1(C - 1))
            nc.vector.tensor_scalar(disd[:, TP:T], dis[:, TP:T], 1.0 / (EDGE * DH_SCALE ** 2), None,
                                    ALU.mult).then_inc(d_free[1], 1)
            widen(0, 0, 1)
            dis_h_low(2)
            widen(0, 0, 2)
            widen(0, 0, 3)
            drop_h1(pro, 0)
            widen(0, 0, 4)
            dve.wait_ge(ssq_ready, C)
            nc.vector.tensor_scalar(pow_in[:, 2, :], ssq[:, :], COS_EPS ** 2, 1.0 / HN_SCALE ** 2,
                                    ALU.max, ALU.mult).then_inc(pow_asked, 1)
            widen(0, 0, 5)
            dis_h_low(C - 1)
            widen(0, 0, 6)
            widen(0, 0, 7)
            beside_diffusion(pro, 0, 1)
            with dve.Fori(1, C) as c:
                chain = Chain(d_step, (c - 1) * 4)
                beside_diffusion(chain, c, 0)
                beside_diffusion(chain, c, 1)
            hnT_low(2 * C, 1)
            take_diffusion(pro, C - 1, 1, 1)
            take_diffusion(pro, C - 1, 1, 0)

            def mask(n, par):
                dve.wait_ge(q_ready, n + 1)
                wait(dve, ylo_ready, n - 1)
                nc.vector.scalar_tensor_tensor(out=wt[:, par, :], in0=area(par), scalar=col(C_E0),
                                               in1=adj8[:, n, :], op0=ALU.subtract, op1=ALU.mult).then_inc(y_ready, 1)

            def y_low(n, par):
                dve.wait_ge(yhi_ready, n + 1)
                nc.vector.scalar_tensor_tensor(out=yp[:, par, 1, :], in0=wt[:, par, :], scalar=Y_SCALE,
                                               in1=yp[:, par, 0, :], op0=ALU.mult,
                                               op1=ALU.subtract).then_inc(ylo_ready, 1)

            def take_sums(c):
                dve.wait_ge(y_used, (c + 1) * T)
                if c >= 1:
                    dve.wait_ge(out_ready, c)
                for k, n in BANKS:
                    ins = nc.vector.tensor_tensor(fin[:, k * BK:k * BK + n, :], accs(4, k, n),
                                                  tot[:, :].unsqueeze(1).broadcast_to([P, n, A]), ALU.add)
                ins.then_inc(acc_free, 1)

            def finish(c):
                dve.wait_ge(acc_free, C + 1 + c)
                pro.link(nc.vector.reciprocal(rden[:, :], fin[:, :, D]))
                pro.link(nc.vector.tensor_scalar(rden[:, :], rden[:, :], col(C_SIG), None, ALU.mult))
                for r in range(R):
                    dst = res[:, c * R + r, :]
                    ins = nc.vector.scalar_tensor_tensor(out=dst, in0=fin[:, r, 0:D], scalar=rden[:, r:r + 1],
                                                         in1=dst, op0=ALU.mult, op1=ALU.add)
                ins.then_inc(out_ready, 1)

            def mask_pair(k):
                mask(2 * k + 1, 1)
                y_low(2 * k, 0)
                mask(2 * k + 2, 0)
                y_low(2 * k + 1, 1)

            dve.wait_ge(scal_ready, 2)
            mask(0, 0)
            mask_pair(0)
            dve.wait_ge(tot_psum, 1)
            nc.vector.tensor_scalar(tot[:, :], ps[:, 7, 0:A], col(C_E0), EDGE * Y_SCALE, ALU.mult, ALU.mult)
            mask_pair(1)
            for c in range(C):
                if c >= 1:
                    mask_pair(c * TP)
                    mask_pair(c * TP + 1)
                with dve.Fori(c * TP + 2, c * TP + 4) as k:
                    mask_pair(k)
                if c >= 1:
                    finish(c - 1)
                with dve.Fori(c * TP + 4, (c + 1) * TP - (c == C - 1)) as k:
                    mask_pair(k)
                if c == C - 1:
                    mask(NT - 1, 1)
                    y_low(NT - 2, 0)
                    y_low(NT - 1, 1)
                take_sums(c)
            for hf in range(2):
                dve.wait_ge(d_free[hf], C + 1)
            finish(C - 1)


def kernel(**inputs):
    import numpy as _np
    import concourse.bacc as _bacc
    from concourse import mybir as _mybir
    from concourse.bass_utils import run_bass_kernel_spmd as _run

    x = _np.ascontiguousarray(inputs["x"])
    n = x.shape[1]
    b = _np.asarray(inputs["L0_gnn_b"])
    W = _np.asarray(inputs["L0_gnn_W"])
    a_s = _np.asarray(inputs["L0_gnn_a_s"])
    columns = [W, _np.broadcast_to(a_s, (n, n)), _np.broadcast_to(b[:, None], (n, n)),
               _np.asarray(inputs["L0_gnn_a_r"]), a_s,
               _np.broadcast_to(_np.asarray(inputs["L1_gnn_alpha"]), (n, 1)),
               _np.broadcast_to(_np.asarray(inputs["L1_gnn_beta"]), (n, 1)),
               _np.broadcast_to(b[None, :], (n, n))]
    arrays = {"x": x, "adjT": _np.asarray(inputs["adj"]).T, "WT": W.T, "params": _np.concatenate(columns, axis=1)}
    arrays = {k: _np.ascontiguousarray(v) for k, v in arrays.items()}
    nc = _bacc.Bacc("TRN2", target_bir_lowering=False, num_devices=1)
    args = [nc.dram_tensor(k, v.shape, _mybir.dt.from_np(v.dtype), kind="ExternalInput").ap()
            for k, v in arrays.items()]
    args.append(nc.dram_tensor("out", x.shape, _mybir.dt.from_np(x.dtype), kind="ExternalOutput").ap())
    gat_then_cosine_diffusion(nc, *args)
    r = _run(nc, [arrays], core_ids=[0])
    return r.results[0]["out"]
```

```python
from contextlib import ExitStack

import concourse.bass as bass
from concourse import mybir

ALU = mybir.AluOpType
ACT = mybir.ActivationFunctionType
F32 = mybir.dt.float32
F16 = mybir.dt.float16
BF16 = mybir.dt.bfloat16
U8 = mybir.dt.uint8
U16 = mybir.dt.uint16
AX = mybir.AxisListType

P = 128
SLOPE = 0.2
LN_EPS = 1e-5
COS_EPS = 1e-8
HN_SCALE = 256.0
DH_SCALE = 1024.0
H_SCALE = 64.0
EDGE = 4.0
Y_SCALE = 16.0


def gat_then_cosine_diffusion(nc, x, adjT, WT, params, out):
    N, D = x.shape
    T = N // P
    CW = 1024
    C = N // CW
    R = CW // P
    HW = CW // 2
    RH = R // 2
    A = D + 1
    BK = 3
    NT = C * T
    SLOTS = 4
    ASLOTS = 4
    TP = T // 2
    assert D == P and N == C * CW
    assert T * EDGE < 256

    def bank(r):
        return r // BK, (r % BK) * A

    BANKS = [(k, min(BK, R - BK * k)) for k in range((R + BK - 1) // BK)]

    def wait(engine, semaphore, value):
        if not (isinstance(value, int) and value <= 0):
            engine.wait_ge(semaphore, value)

    with ExitStack() as ctx:
        def sb(name, shape, dt=F32):
            return ctx.enter_context(nc.sbuf_tensor(name, shape, dt))

        def sem(name):
            return ctx.enter_context(nc.semaphore(name))

        adj8 = sb("adj8", [P, NT, CW], U8)
        stage = sb("stage", [P, SLOTS, CW])
        cbuf = sb("cbuf", [P, T * A])
        gbuf = sb("gbuf", [P, T, A])
        res = sb("res", [P, T, D])
        wt = sb("wt", [P, 2, CW])
        degs = sb("degs", [P, 2, HW], U16)
        degb = sb("degb", [P, CW], BF16)
        ident = sb("ident", [P, P])
        ones = sb("ones", [1, P])
        ones16 = sb("ones16", [P, P], F16)
        onesb = sb("onesb", [P, 2], BF16)
        hcol = sb("hcol", [P, R], F16)
        bst = sb("bst", [P, R, 6])
        mv = sb("mv", [P, 2, R, 2])
        pow_in = sb("pow_in", [P, 3, T])
        rstd = sb("rstd", [P, T])
        dis = sb("dis", [P, T])
        invn = sb("invn", [P, T])
        half = sb("half", [P, T])
        nmr = sb("nmr", [P, T])
        ssq = sb("ssq", [P, T])
        disd = sb("disd", [P, T])
        vj = sb("vj", [P, T])
        gj = sb("gj", [P, T])
        rden = sb("rden", [P, R])
        sc = sb("sc", [P, 16])

        (C_RMAX, C_RTOP, C_M8R, C_M2R, C_MBS, C_BAS, C_EMA, C_SIG, C_MSIG,
         C_BSC, C_NB, C_E0, C_AS, C_T) = range(14)

        def col(k):
            return sc[:, k:k + 1]

        def row(ap, t):
            return ap[:, bass.ds(t, 1), :].squeeze(1)

        def flat(ap):
            return ap.rearrange("p a b -> p (a b)")

        SHIFT = 16
        cb = cbuf[:, SHIFT:SHIFT + N]
        h1 = cbuf[:, SHIFT:SHIFT + N].rearrange("p (t d) -> p t d", d=D)
        hp = cbuf[:, :].bitcast(F16)[:, 0:T * (2 * D + 1)].rearrange("p (t a) -> p t a", a=2 * D + 1)
        late = flat(adj8[:, NT - T:NT, :]).bitcast(F32)
        h0T = late[:, 0:T * D]
        h0 = late[:, T * D:2 * T * D].rearrange("p (t d) -> p t d", d=D)
        wt3 = flat(adj8[:, NT - 4:NT, :]).bitcast(F32)
        wk = flat(adj8[:, NT - T - 4:NT - T, :]).bitcast(F32)
        par_sb = wk[:, 0:4 * P + 4]
        w_sb, as_sb, bc_sb = wk[:, 0:P], wk[:, P:2 * P], wk[:, 2 * P:3 * P]
        ar_as = wk[:, 3 * P:3 * P + 2]
        alpha, beta = wk[:, 3 * P + 2:3 * P + 3], wk[:, 3 * P + 3:3 * P + 4]
        brow = wk[:, 3 * P + 4:4 * P + 5]
        wtr = wk[:, 4 * P + 8:4 * P + 8 + A]
        ws_sb = wk[:, 6 * P:7 * P]
        adj_pairs = flat(adj8[:, :, :]).bitcast(U16).rearrange("p (n i) -> p n i", i=HW)
        dh = flat(stage[:, :, :]).bitcast(F16).rearrange("p (t k d) -> p t k d", k=2, d=D)
        yp = flat(stage[:, 0:2, :]).bitcast(F16).rearrange("p (b k i) -> p b k i", b=2, k=2)
        fin = flat(stage[:, 2:4, :])[:, 0:R * A].rearrange("p (r a) -> p r a", a=A)
        hnT = flat(gbuf[:, :, :])[:, 0:N].bitcast(F16).rearrange("p (k i) -> p k i", k=2)
        hn = flat(degs[:, :, :]).bitcast(F32).rearrange("p (t d) -> p t d", d=D)
        tot = degb[:, :].bitcast(F32)[:, 0:A]
        a16 = flat(wt[:, :, :]).bitcast(BF16).rearrange("p (s i) -> p s i", s=2 * ASLOTS)
        hparts = wt[:, 1, :].bitcast(F16).rearrange("p (k t d) -> p k t d", k=2, d=D)

        ps = ctx.enter_context(nc.psum_tensor("ps", [P, 8, 512], F32))

        def area(k):
            return flat(ps[:, 2 * k:2 * k + 2, :])

        def first_bank(c):
            return 4 * (c % 2)

        def acc(fb, r, width):
            b, o = bank(r)
            return ps[:, fb + b, o:o + width]

        def accs(fb, k, n):
            return ps[:, fb + k, 0:n * A].rearrange("p (r a) -> p r a", a=A)

        THIRD_UNTIL = 14

        def buffers(n):
            return 3 if n < (C - 1) * T + THIRD_UNTIL else 2

        def weights(n):
            b = n % buffers(n)
            return wt3 if b == 2 else wt[:, b, :]

        x_loaded = [sem(f"x_loaded{q}") for q in range(C)]
        w_loaded = sem("w_loaded")
        stage_loaded = [sem(f"stage_loaded{s}") for s in range(SLOTS)]
        adj_kept = sem("adj_kept")
        consts_ready = sem("consts_ready")
        pow_asked = sem("pow_asked")
        pow_done = sem("pow_done")
        dve_step = sem("dve_step")
        wprod_ready = sem("wprod_ready")
        wprod_kept = sem("wprod_kept")
        nmr_ready = sem("nmr_ready")
        h0_ready = [sem(f"h0_ready{q}") for q in range(C)]
        h0T_psum = sem("h0T_psum")
        h0T_ready = sem("h0T_ready")
        H_psum = sem("H_psum")
        H_kept = sem("H_kept")
        s_psum = sem("s_psum")
        rmax_part = sem("rmax_part")
        rmax_row = sem("rmax_row")
        rmax_one = sem("rmax_one")
        rmax_all = sem("rmax_all")
        shift_ready = sem("shift_ready")
        vg_ready = sem("vg_ready")
        c_raw = sem("c_raw")
        scal_ready = sem("scal_ready")
        g_ready = sem("g_ready")
        c_ready = sem("c_ready")
        p_ready = sem("p_ready")
        p_used = sem("p_used")
        count_step = sem("count_step")
        degb_ready = sem("degb_ready")
        deg_psum = sem("deg_psum")
        acc_free = sem("acc_free")
        h1_ready = sem("h1_ready")
        ssq_ready = sem("ssq_ready")
        dh_hi = sem("dh_hi")
        dh_lo = sem("dh_lo")
        a16_dve = sem("a16_dve")
        a16_act = sem("a16_act")
        a16_used = sem("a16_used")
        d_free = [sem(f"d_free{k}") for k in range(2)]
        d_step = sem("d_step")
        hn_ready = sem("hn_ready")
        hnT_psum = sem("hnT_psum")
        hnT_hi = sem("hnT_hi")
        hnT_lo = sem("hnT_lo")
        hp_hi = sem("hp_hi")
        hp_ready = sem("hp_ready")
        tot_psum = sem("tot_psum")
        z_ready = sem("z_ready")
        q_ready = sem("q_ready")
        y_ready = sem("y_ready")
        yhi_ready = sem("yhi_ready")
        ylo_ready = sem("ylo_ready")
        y_used = sem("y_used")
        sums_ready = sem("sums_ready")
        sums_kept = sem("sums_kept")
        out_ready = sem("out_ready")
        stored = sem("stored")

        xt = x.rearrange("(t p) d -> p t d", p=P)
        ot = out.rearrange("(t p) d -> p t d", p=P)
        at = adjT.rearrange("(t p) (c i) -> c t p i", p=P, i=CW)

        POW_LN0 = [q + 1 for q in range(C)]

        def POW_DIS(c):
            return C + 2 * c + 1

        def POW_LN1(c):
            return C + 2 * c + 2

        POW_NORM = (3 * C + 1, 3 * C + 2)

        FIRST_GROUPS = [(hf, 2 * q + g) for q in range(T // (2 * ASLOTS)) for hf in range(2) for g in range(2)]
        FIRST_DONE = [ASLOTS * (1 + max(k for k, (h, _) in enumerate(FIRST_GROUPS) if h == hf)) for hf in range(2)]

        def last(c):
            return isinstance(c, int) and c == C - 1


        def a16_slot(c, hf, g, s, place):
            if place is None:
                return s, (2 * c + hf) * T + g * ASLOTS + s - (ASLOTS - 1)
            return (place % 2) * ASLOTS + s, (place - 2) * ASLOTS + s + 1

        H_BANK = (4, 4, 0, 4)

        G_PARTS = [(0, 2), (2, R)] + [(q * R, (q + 1) * R) for q in range(1, C)]

        block = ctx.enter_context(nc.Block())

        @block.sync
        def _(sp):
            sp.dma_start(par_sb, params).then_inc(w_loaded, 16)
            sp.dma_start(wtr[:, 0:D], WT).then_inc(w_loaded, 16)
            for q in range(C):
                sp.dma_start(res[:, q * R:(q + 1) * R, :], xt[:, q * R:(q + 1) * R, :]).then_inc(x_loaded[q], 16)

            def load(c, g, first):
                for s in range(SLOTS):
                    if not first:
                        sp.wait_ge(adj_kept, c * T + g * SLOTS + s - (SLOTS - 1))
                    sp.dma_start(stage[:, s, :], at[c, g * SLOTS + s]).then_inc(stage_loaded[s], 16)

            load(0, 0, True)
            with sp.Fori(1, T // SLOTS) as g:
                load(0, g, False)
            with sp.Fori(1, C) as c:
                with sp.Fori(0, T // SLOTS) as g:
                    load(c, g, False)
            pieces = [(c * R, (c + 1) * R) for c in range(C - 1)] + [(T - R, T - RH), (T - RH, T)]
            for k, (t0, t1) in enumerate(pieces):
                sp.wait_ge(out_ready, k + 1)
                sp.dma_start(ot[:, t0:t1, :], res[:, t0:t1, :]).then_inc(stored, 16)
            sp.wait_ge(stored, 16 * len(pieces))

        @block.gpsimd
        def _(pool):
            pool.memset(ident[:, :], 0.0).then_inc(consts_ready, 1)
            pool.memset(half[:, :], -0.5).then_inc(consts_ready, 1)
            pool.memset(ones[:, :], 1.0).then_inc(consts_ready, 1)
            pool.memset(ones16[:, :], 1.0).then_inc(consts_ready, 1)
            pool.memset(onesb[:, :], 1.0).then_inc(consts_ready, 1)
            pool.memset(hcol[:, :], H_SCALE).then_inc(consts_ready, 1)
            pool.wait_ge(consts_ready, 6)
            pool.affine_select(out=ident[:, :], in_=ident[:, :], compare_op=ALU.not_equal, fill=1.0, base=0,
                               pattern=[[-1, P]], channel_multiplier=1).then_inc(consts_ready, 1)
            chunk_cols = [slice(q * R, (q + 1) * R) for q in range(C)]
            asks = [(rstd, 0, w) for w in chunk_cols]
            for w in chunk_cols:
                asks += [(dis, 1, w), (rstd, 0, w)]
            asks += [(invn, 2, slice(0, T - R)), (invn, 2, chunk_cols[-1])]
            for k, (dst, src, w) in enumerate(asks):
                pool.wait_ge(pow_asked, k + 1)
                nc.gpsimd.tensor_tensor(dst[:, w], pow_in[:, src, w], half[:, w], ALU.pow).then_inc(pow_done, 1)

        @block.scalar
        def _(act):
            def normalize(dst, t):
                return nc.scalar.activation(dst, res[:, t, :], ACT.Relu, bias=nmr[:, t:t + 1], scale=rstd[:, t:t + 1])

            act.wait_ge(wprod_ready, 1)
            nc.scalar.activation(wtr[:, D:A], ps[:, 7, 128:129], ACT.Copy).then_inc(wprod_kept, 1)
            nc.scalar.activation(brow[:, D:A], ps[:, 7, 130:131], ACT.Copy).then_inc(wprod_kept, 1)
            nc.scalar.activation(col(C_BAS), ps[:, 7, 131:132], ACT.Copy).then_inc(wprod_kept, 1)
            nc.scalar.activation(ws_sb, ps[:, 7, 0:P], ACT.Copy).then_inc(wprod_kept, 1)
            nc.scalar.activation(col(C_EMA), alpha, ACT.Exp, scale=-1.0).then_inc(scal_ready, 1)
            def keep(g, slots=range(SLOTS)):
                for s in slots:
                    act.wait_ge(stage_loaded[s], 16 * g + 16)
                    nc.scalar.activation(adj8[:, g * SLOTS + s, :], stage[:, s, :], ACT.Copy,
                                         scale=EDGE).then_inc(adj_kept, 1)

            def norm0(q):
                act.wait_ge(nmr_ready, q + 1)
                for t in range(q * R, (q + 1) * R):
                    ins = normalize(h0[:, t, :], t)
                ins.then_inc(h0_ready[q], 1)

            def keep_h0T(q):
                act.wait_ge(h0T_psum, q + 1)
                nc.scalar.activation(h0T[:, q * CW:(q + 1) * CW], area(q % 2), ACT.Copy).then_inc(h0T_ready, 1)

            norm0(0)
            keep(0, (0,))
            keep_h0T(0)
            norm0(1)
            keep(0, (1,))
            keep_h0T(1)
            keep_h0T(2)
            keep(0, (2, 3))
            keep_h0T(3)
            keep(1)
            act.wait_ge(shift_ready, 1)

            def c_exp(q):
                act.wait_ge(s_psum, q + 1)
                nc.scalar.activation(cb[:, q * CW:(q + 1) * CW], area(0 if q == 0 else 2), ACT.Exp, bias=col(C_MBS),
                                     scale=-(1 - SLOPE)).then_inc(c_raw, 1)

            GC = T // SLOTS
            c_exp(0)
            nc.scalar.activation(gj[:, :], gbuf[:, :, D], ACT.Exp, bias=col(C_M2R), scale=SLOPE).then_inc(vg_ready, 1)
            nc.scalar.activation(vj[:, :], gbuf[:, :, D], ACT.Exp, bias=col(C_M8R),
                                 scale=1 - SLOPE).then_inc(vg_ready, 1)
            nc.scalar.activation(col(C_E0), col(C_NB), ACT.Exp).then_inc(scal_ready, 1)
            for q in range(1, C):
                with act.Fori(3 * q - 1, 3 * q + 2) as g:
                    keep(g)
                c_exp(q)

            def norm1(c, rows=range(R)):
                act.wait_ge(nmr_ready, 3 + c)
                for r in rows:
                    ins = normalize(h1[:, c * R + r, :], c * R + r)
                if R - 1 in rows:
                    ins.then_inc(h1_ready, 1)

            AHEAD = 5
            with act.Fori(3 * C - 1, GC + AHEAD) as g:
                keep(g)
            act.wait_ge(g_ready, len(G_PARTS))
            for c in range(C - 1):
                norm1(c)
                with act.Fori((c + 1) * GC + AHEAD, min((c + 2) * GC + AHEAD, C * GC - 1)) as g:
                    keep(g)
            act.wait_ge(p_used, (C - 1) * T + THIRD_UNTIL)
            keep(C * GC - 1)

            def dis_h(q, rows=range(R)):
                act.wait_ge(pow_done, POW_DIS(q))
                for r in rows:
                    t = q * R + r
                    ins = nc.scalar.activation(dh[:, t, 0, :], h1[:, t, :], ACT.Copy, scale=dis[:, t:t + 1])
                if R - 1 in rows:
                    ins.then_inc(dh_hi, 1)

            def squares(q):
                act.wait_ge(h1_ready, q + 1)
                if q >= 1:
                    act.wait_ge(ssq_ready, q)
                squared = area(1 if q < C - 1 else 2)
                for t in range(R):
                    ins = nc.scalar.activation(squared[:, t * D:(t + 1) * D], h1[:, q * R + t, :], ACT.Square,
                                               accum_out=ssq[:, q * R + t:q * R + t + 1])
                ins.then_inc(ssq_ready, 1)

            act.wait_ge(adj_kept, NT)
            for q in range(C - 1):
                dis_h(q)
            act.wait_ge(acc_free, C - 1)
            for q in range(C - 1):
                squares(q)

            def widen(c, hf, g, place=None):
                for s in range(ASLOTS // 2, ASLOTS):
                    slot, used = a16_slot(c, hf, g, s, place)
                    wait(act, a16_used, used)
                    nc.scalar.activation(a16[:, slot, :], adj8[:, c * T + g * ASLOTS + s, hf * HW:(hf + 1) * HW],
                                         ACT.Copy).then_inc(a16_act, 1)

            def make_hn(c, hf):
                for t in range(RH):
                    tile = c * R + hf * RH + t
                    ins = nc.scalar.activation(hn[:, t, :], row(h1, tile), ACT.Copy, scale=invn[:, bass.ds(tile, 1)])
                ins.then_inc(hn_ready, 1)

            def hnT_high(sub, hf):
                act.wait_ge(hnT_psum, sub)
                w = bass.ds((sub - 1) * HW, HW)
                nc.scalar.activation(hnT[:, 0, w], ps[:, 4 + hf, :], ACT.Copy).then_inc(hnT_hi, 1)

            def high_hp(c):
                nc.scalar.activation(hparts[:, 0, :, :], h1[:, bass.ds(c * R, R), :], ACT.Copy,
                                     scale=H_SCALE).then_inc(hp_hi, 1)

            def beside_diffusion(c, hf):
                widen(c, hf, 0)
                hnT_high(2 * c + hf, 1 - hf)
                for g in range(1, GC):
                    widen(c, hf, g)
                    if g == 3:
                        make_hn(c, hf)
                    if g == 4 and hf == 0:
                        high_hp(c - 1)
                    if g == 4 and hf == 1 and last(c):
                        high_hp(c)

            for place, (hf, g) in enumerate(FIRST_GROUPS):
                if place < 2:
                    act.wait_ge(p_used, NT - 1 + place)
                if place == 6:
                    norm1(C - 1, range(R // 2))
                if place == 7:
                    norm1(C - 1, range(R // 2, R))
                if place == 8:
                    act.wait_ge(h1_ready, C)
                    dis_h(C - 1, range(R // 2))
                if place == 9:
                    dis_h(C - 1, range(R // 2, R))
                if place == 10:
                    squares(C - 1)
                if place == 11:
                    act.wait_ge(pow_done, POW_NORM[0])
                    act.wait_ge(degb_ready, C)
                    make_hn(0, 0)
                widen(0, hf, g, place)
            hnT_high(1, 0)
            make_hn(0, 1)
            act.wait_ge(pow_done, POW_NORM[1])
            with act.Fori(1, C - 1) as c:
                beside_diffusion(c, 0)
                beside_diffusion(c, 1)
            beside_diffusion(C - 1, 0)
            beside_diffusion(C - 1, 1)
            hnT_high(2 * C, 1)

            def expo(n, par):
                act.wait_ge(z_ready, n + 1)
                nc.scalar.activation(area(par), area(par), ACT.Exp, bias=col(C_NB),
                                     scale=col(C_BSC)).then_inc(q_ready, 1)

            def y_high(n, par):
                act.wait_ge(y_ready, n + 1)
                wait(act, y_used, n - 1)
                nc.scalar.activation(yp[:, par, 0, :], wt[:, par, :], ACT.Copy,
                                     scale=Y_SCALE).then_inc(yhi_ready, 1)

            act.wait_ge(a16_used, 2 * NT)
            expo(0, 0)
            expo(1, 1)
            y_high(0, 0)
            expo(2, 0)
            y_high(1, 1)

            def keep_sums(c):
                wait(act, out_ready, c)
                for k, n in BANKS:
                    if k < len(BANKS) - 1:
                        act.wait_ge(sums_ready, c * (len(BANKS) - 1) + k + 1)
                    else:
                        act.wait_ge(y_used, (c + 1) * T)
                    nc.scalar.activation(fin[:, k * BK:k * BK + n, :], accs(4, k, n), ACT.Copy).then_inc(sums_kept, 1)

            for c in range(C):
                if c >= 1:
                    expo(c * T + 1, 1)
                    y_high(c * T, 0)
                    expo(c * T + 2, 0)
                    keep_sums(c - 1)
                    y_high(c * T + 1, 1)
                with act.Fori(c * TP + 1, (c + 1) * TP - (c == C - 1)) as k:
                    expo(2 * k + 1, 1)
                    y_high(2 * k, 0)
                    expo(2 * k + 2, 0)
                    y_high(2 * k + 1, 1)
            expo(NT - 1, 1)
            y_high(NT - 2, 0)
            y_high(NT - 1, 1)

        @block.tensor
        def _(pe):
            pe.wait_ge(w_loaded, 16 * 2)
            pe.matmul(ps[:, 7, 0:P], w_sb, as_sb, start=True, stop=True)
            pe.matmul(ps[:, 7, 128:129], w_sb, ar_as[:, 0:1], start=True, stop=True)
            pe.matmul(ps[:, 7, 130:132], bc_sb, ar_as, start=True, stop=True).then_inc(wprod_ready, 1)
            pe.wait_ge(consts_ready, 7)

            def keep_clock(n):
                for _ in range(n):
                    pe.matmul(ps[:, 3, 0:P], ones16[:, :], ones16[:, :], start=True, stop=True)

            def turn_h0(q):
                pe.wait_ge(h0_ready[q], 1)
                if q >= 2:
                    pe.wait_ge(h0T_ready, q - 1)
                for t in range(R):
                    mm = pe.transpose(area(q % 2)[:, t * P:(t + 1) * P], h0[:, q * R + t, :], ident[:, :])
                mm.then_inc(h0T_psum, 1)

            def project(q):
                pe.wait_ge(h0T_ready, q + 1)
                if q == 0:
                    pe.wait_ge(wprod_kept, 4)
                if q == 2:
                    pe.wait_ge(h0T_ready, C)
                elif q >= 1:
                    pe.wait_ge(H_kept, (q + 1) // 2)
                for t in range(R):
                    mm = pe.matmul(acc(H_BANK[q], t, A), h0T[:, (q * R + t) * P:(q * R + t + 1) * P], wtr,
                                   start=True, stop=True)
                mm.then_inc(H_psum, 1)

            def scores(q, parts=range(CW // 512)):
                for f in parts:
                    mm = pe.matmul(ps[:, (0 if q == 0 else 4) + f, :], ws_sb,
                                   h0T[:, q * CW + f * 512:q * CW + (f + 1) * 512], start=True, stop=True)
                if CW // 512 - 1 in parts:
                    mm.then_inc(s_psum, 1)

            keep_clock(110)
            turn_h0(0)
            project(0)
            turn_h0(1)
            turn_h0(2)
            project(1)
            turn_h0(3)
            project(2)
            project(3)
            pe.wait_ge(H_kept, 3)
            scores(0, (0,))
            pe.wait_ge(rmax_part, 1)
            pe.transpose(ps[0:1, 7, 256:256 + P], col(C_RMAX), ident[:, :]).then_inc(rmax_row, 1)
            scores(0, (1,))
            pe.wait_ge(rmax_one, 1)
            pe.matmul(ps[:, 7, 400:401], ones[:, :], sc[0:1, C_RTOP:C_RTOP + 1],
                      start=True, stop=True).then_inc(rmax_all, 1)
            keep_clock(70)

            def attend(c, k, k0=0):
                fb = first_bank(c)
                for t in (2 * k, 2 * k + 1):
                    n = c * T + t
                    pe.wait_ge(p_ready, 2 * k0 + n + 1)
                    for r in range(R):
                        mm = pe.matmul(acc(fb, r, A), weights(n)[:, r * P:(r + 1) * P], row(gbuf, 2 * k0 + t),
                                       start=t == 0 and isinstance(k0, int) and r % BK == 0, stop=False,
                                       skip_group_check=True)
                    mm.then_inc(p_used, 1)

            def attend_three(c, k, k0=0):
                for m in range(k, k + 3):
                    attend(c, m, k0)

            def degrees(c):
                pe.wait_ge(degb_ready, c + 1)
                for r in range(R):
                    mm = pe.matmul(ps[:, first_bank(c) + 3, r:r + 1], degb[:, r * P:(r + 1) * P], onesb[:, 0:1],
                                   start=r == 0, stop=r == R - 1, skip_group_check=True)
                mm.then_inc(deg_psum, 1)

            for c in range(C):
                if c == 0:
                    pe.wait_ge(g_ready, 1)
                    attend(0, 0)
                    scores(1)
                    pe.wait_ge(g_ready, 2)
                    for k in range(1, 4):
                        attend(0, k)
                    for q in range(2, C):
                        pe.wait_ge(g_ready, q + 1)
                        attend_three(0, 4 + 3 * (q - 2))
                        pe.wait_ge(c_raw, q)
                        scores(q)
                    pe.wait_ge(g_ready, len(G_PARTS))
                    done = 4 + 3 * (C - 2)
                else:
                    if c == 1:
                        pe.wait_ge(c_raw, C)
                    else:
                        pe.wait_ge(acc_free, c - 1)
                    for k in range(4):
                        attend(c, k)
                        if k == 1:
                            degrees(c - 1)
                    done = 4
                    if c == C - 1:
                        attend_three(c, done)
                        done = THIRD_UNTIL // 2
                with pe.Fori(0, (TP - done) // 3) as kk:
                    attend_three(c, done, 3 * kk)
            degrees(C - 1)

            def diffuse(c, hf, t, place=None):
                s = t % ASLOTS
                if place is None:
                    slot, before = s, (2 * c + hf) * (T // 2) + (t - s) // 2
                else:
                    slot, before = (place % 2) * ASLOTS + s, place * (ASLOTS // 2)
                pe.wait_ge(a16_dve if s < ASLOTS // 2 else a16_act, before + s % (ASLOTS // 2) + 1)
                if t % R == 0:
                    pe.wait_ge(dh_lo, t // R + 1)
                for r in range(RH):
                    mm = pe.matmul(ps[:, 2 * hf + r // 2, (r % 2) * 2 * D:(r % 2 + 1) * 2 * D],
                                   a16[:, slot, r * P:(r + 1) * P], dh[:, t, :, :].rearrange("p k d -> p (k d)"),
                                   start=t == 0 and r % 2 == 0, stop=t == T - 1, skip_group_check=True)
                mm.then_inc(a16_used, 1)

            def turn_hn(c, hf):
                pe.wait_ge(hn_ready, 2 * c + hf + 1)
                for t in range(RH):
                    mm = pe.transpose(ps[:, 4 + hf, t * P:(t + 1) * P], hn[:, t, :], ident[:, :])
                mm.then_inc(hnT_psum, 1)

            def diffuse_half(c, hf):
                pe.wait_ge(d_free[hf], c)
                for t in range(T - ASLOTS):
                    diffuse(c, hf, t)
                turn_hn(c, hf)
                for t in range(T - ASLOTS, T):
                    diffuse(c, hf, t)

            pe.wait_ge(acc_free, C - 1)
            pe.wait_ge(ssq_ready, C - 1)
            for k, (hf, g) in enumerate(FIRST_GROUPS):
                for s in range(ASLOTS):
                    diffuse(0, hf, g * ASLOTS + s, k)
                if g == T // ASLOTS - 1:
                    turn_hn(0, hf)
            with pe.Fori(1, C) as c:
                diffuse_half(c, 0)
                diffuse_half(c, 1)

            def cosine(c, t, n, par):
                wait(pe, y_ready, n - 1)
                if isinstance(n, int) and n < 2:
                    pe.wait_ge(d_free[par], C)
                for a, b in ((0, 0), (0, 1), (1, 0)):
                    for f in range(CW // 512):
                        mm = pe.matmul(ps[:, 2 * par + f, :], hnT[:, a, bass.ds(t * P, P)],
                                       hnT[:, b, bass.ds(c * CW + f * 512, 512)],
                                       start=(a, b) == (0, 0), stop=a == 1, skip_group_check=True)
                mm.then_inc(z_ready, 1)

            def weigh(t, n, par, c=None):
                first, last = c is not None and t == 0, c is not None and t == T - 1
                pe.wait_ge(ylo_ready, n + 1)
                for r in range(R):
                    if first and r % BK == 0:
                        wait(pe, sums_kept, ((c - 1) * len(BANKS) + r // BK + 1) if c >= 1 else 0)
                    hi, lo = (yp[:, par, k, r * P:(r + 1) * P] for k in range(2))
                    pe.matmul(acc(4, r, A), hi, hp[:, t, 0:A], start=first and r % BK == 0, stop=False,
                              skip_group_check=True)
                    pe.matmul(acc(4, r, D), hi, hp[:, t, A:A + D], start=False, stop=False, skip_group_check=True)
                    mm = pe.matmul(acc(4, r, A), lo, hp[:, t, 0:A], start=False, stop=False, skip_group_check=True)
                    if last and r % BK == BK - 1:
                        mm.then_inc(sums_ready, 1)
                mm.then_inc(y_used, 1)

            def sum_h1(tiles):
                for t in tiles:
                    pe.matmul(ps[:, 7, 0:A], ones16[:, :], hp[:, t, 0:A], start=(t == 0), stop=False,
                              skip_group_check=True)
                    mm = pe.matmul(ps[:, 7, 0:D], ones16[:, :], hp[:, t, A:A + D], start=False, stop=(t == T - 1),
                                   skip_group_check=True)
                if T - 1 in tiles:
                    mm.then_inc(tot_psum, 1)

            cosine(0, 0, 0, 0)
            pe.wait_ge(hp_ready, C)
            sum_h1(range(10))
            cosine(0, 1, 1, 1)
            sum_h1(range(10, T))
            pe.wait_ge(hnT_lo, 2 * C)
            cosine(0, 2, 2, 0)
            AHEAD = 3
            for c in range(C):
                for t in range(4):
                    n = c * T + t
                    cosine(c, t + AHEAD, n + AHEAD, (t + AHEAD) % 2)
                    weigh(t, n, t % 2, c)
                with pe.Fori(1, T // 4 - 1) as g:
                    for s in range(4):
                        cosine(c, 4 * g + s + AHEAD, c * T + 4 * g + s + AHEAD, (s + AHEAD) % 2)
                        weigh(4 * g + s, c * T + 4 * g + s, s % 2)
                for t in range(T - 4, T):
                    n = c * T + t
                    if t + AHEAD < T:
                        cosine(c, t + AHEAD, n + AHEAD, (t + AHEAD) % 2)
                    elif c + 1 < C:
                        cosine(c + 1, t + AHEAD - T, n + AHEAD, (t + AHEAD) % 2)
                    weigh(t, n, t % 2, c)

        @block.vector
        def _(dve):
            class Chain:
                def __init__(self, semaphore, base=0):
                    self.semaphore, self.base, self.k = semaphore, base, 0

                def link(self, ins):
                    self.k += 1
                    ins.then_inc(self.semaphore, 1)
                    dve.wait_ge(self.semaphore, self.base + self.k)

            pro = Chain(dve_step)

            def row_stats(c, rows):
                for t in rows:
                    ins = nc.vector.bn_stats(bst[:, t, :], res[:, c * R + t, :])
                pro.link(ins)

            def ask_rstd(c, m=0):
                for t in range(R):
                    ins = nc.vector.bn_aggr(mv[:, m, t, :], bst[:, t, :])
                pro.link(ins)
                nc.vector.tensor_scalar(pow_in[:, 0, c * R:(c + 1) * R], mv[:, m, :, 1], LN_EPS, None,
                                        ALU.add).then_inc(pow_asked, 1)

            def statistics(c, m=0):
                row_stats(c, range(R))
                ask_rstd(c, m)

            def mean_shift(c, answer, m=0):
                dve.wait_ge(pow_done, answer)
                w = slice(c * R, (c + 1) * R)
                nc.vector.scalar_tensor_tensor(out=nmr[:, w], in0=mv[:, m, :, 0], scalar=-1.0, in1=rstd[:, w],
                                               op0=ALU.mult, op1=ALU.mult).then_inc(nmr_ready, 1)

            def center(q, m):
                w = slice(q * R, (q + 1) * R)
                pro.link(nc.vector.tensor_tensor(h0[:, w, :], res[:, w, :],
                                                 mv[:, m, :, 0:1].broadcast_to([P, R, D]), ALU.subtract))

            def norm0(q):
                dve.wait_ge(pow_done, POW_LN0[q])
                w = slice(q * R, (q + 1) * R)
                nc.vector.scalar_tensor_tensor(
                    out=h0[:, w, :], in0=h0[:, w, :], scalar=0.0, in1=rstd[:, w].unsqueeze(2).broadcast_to([P, R, D]),
                    op0=ALU.max, op1=ALU.mult).then_inc(h0_ready[q], 1)

            def keep_H(q):
                dve.wait_ge(H_psum, q + 1)
                for k, n in BANKS:
                    t0 = q * R + k * BK
                    ins = nc.vector.tensor_tensor(gbuf[:, t0:t0 + n, :], accs(H_BANK[q], k, n),
                                                  brow.unsqueeze(1).broadcast_to([P, n, A]), ALU.add)
                ins.then_inc(H_kept, 1)

            dve.wait_ge(x_loaded[0], 16)
            statistics(0, 0)
            dve.wait_ge(x_loaded[1], 16)
            statistics(1, 1)
            mean_shift(0, POW_LN0[0], 0)
            dve.wait_ge(x_loaded[2], 16)
            statistics(2, 0)
            mean_shift(1, POW_LN0[1], 1)
            dve.wait_ge(x_loaded[3], 16)
            statistics(3, 1)
            center(2, 0)
            norm0(2)
            center(3, 1)
            norm0(3)
            dve.wait_ge(wprod_kept, 4)
            keep_H(0)
            dve.wait_ge(scal_ready, 1)
            pro.link(nc.vector.tensor_scalar(col(C_T), col(C_EMA), 1.0, None, ALU.add))
            pro.link(nc.vector.reciprocal(col(C_SIG), col(C_T)))
            nc.vector.tensor_scalar(col(C_MSIG), col(C_SIG), -1.0, -1.0, ALU.mult, ALU.add)
            nc.vector.tensor_scalar(col(C_BSC), beta, 1.0 / HN_SCALE ** 2, None, ALU.mult)
            nc.vector.scalar_tensor_tensor(out=col(C_NB), in0=beta, scalar=-1.0, in1=beta, op0=ALU.mult, op1=ALU.min)
            pro.link(nc.vector.tensor_scalar(col(C_AS), col(C_BAS), -(1 - SLOPE), None, ALU.mult))
            for q in range(1, C - 1):
                keep_H(q)
            dve.wait_ge(H_psum, C)
            for k, n in BANKS:
                t0 = (C - 1) * R + k * BK
                ins = nc.vector.tensor_tensor(gbuf[:, t0:t0 + n, D], accs(H_BANK[-1], k, n)[:, :, D],
                                              brow[:, D:A].broadcast_to([P, n]), ALU.add)
            pro.link(ins)
            nc.vector.tensor_reduce(col(C_RMAX), gbuf[:, :, D], AX.X, ALU.max).then_inc(rmax_part, 1)

            def keep_last(k, n):
                t0 = (C - 1) * R + k * BK
                return nc.vector.tensor_tensor(gbuf[:, t0:t0 + n, 0:D], accs(H_BANK[-1], k, n)[:, :, 0:D],
                                               brow[:, 0:D].unsqueeze(1).broadcast_to([P, n, D]), ALU.add)

            keep_last(*BANKS[0])
            dve.wait_ge(rmax_row, 1)
            nc.vector.tensor_reduce(sc[0:1, C_RTOP:C_RTOP + 1], ps[0:1, 7, 256:256 + P], AX.X,
                                    ALU.max).then_inc(rmax_one, 1)
            keep_last(*BANKS[1])
            dve.wait_ge(rmax_all, 1)
            nc.vector.tensor_scalar(col(C_M2R), ps[:, 7, 400:401], -SLOPE, None, ALU.mult)
            pro.link(nc.vector.tensor_scalar(col(C_M8R), ps[:, 7, 400:401], -(1 - SLOPE), None, ALU.mult))
            nc.vector.tensor_tensor(col(C_MBS), col(C_AS), col(C_M8R), ALU.add).then_inc(shift_ready, 1)
            keep_last(*BANKS[2]).then_inc(H_kept, 1)

            def scale_H(part):
                t0, t1 = G_PARTS[part]
                nc.vector.tensor_tensor(gbuf[:, t0:t1, 0:D], gbuf[:, t0:t1, 0:D],
                                        gj[:, t0:t1].unsqueeze(2).broadcast_to([P, t1 - t0, D]), ALU.mult)
                nc.vector.tensor_copy(gbuf[:, t0:t1, D], gj[:, t0:t1]).then_inc(g_ready, 1)

            def cap_c(q):
                dve.wait_ge(c_raw, q + 1)
                w = slice(q * CW, (q + 1) * CW)
                nc.vector.tensor_scalar(cb[:, w], cb[:, w], 1.0, None, ALU.min).then_inc(c_ready, 1)

            def edge_weights(c, t, t0=0):
                n = c * T + t
                dve.wait_ge(adj_kept, t0 + n + 1)
                wait(dve, p_used, t0 + n + 1 - buffers(n))
                nc.vector.scalar_tensor_tensor(out=weights(n), in0=cb[:, c * CW:(c + 1) * CW],
                                               scalar=vj[:, bass.ds(t0 + t, 1)], in1=row(adj8, t0 + n),
                                               op0=ALU.max, op1=ALU.mult).then_inc(p_ready, 1)

            def count_edges(c, k, k0=0):
                m = k0 + c * TP + k
                if isinstance(k0, int) and k == 0:
                    return
                if isinstance(k0, int) and k == 1:
                    wait(dve, degb_ready, c)
                    before = adj_pairs[:, 2 * m - 2:2 * m, :]
                else:
                    dve.wait_ge(count_step, m - 1)
                    before = degs[:, :, :]
                nc.vector.tensor_tensor(degs[:, :, :], before, adj_pairs[:, bass.ds(2 * m, 2), :],
                                        ALU.add).then_inc(count_step, 1)

            def sum_counts(c):
                dve.wait_ge(count_step, (c + 1) * TP - 1)
                wait(dve, deg_psum, c)
                even, odd = (degs[:, k, :].bitcast(U8) for k in range(2))
                nc.vector.tensor_tensor(degb[:, :], even, odd, ALU.add).then_inc(degb_ready, 1)
                dve.sem_inc(count_step, 1)

            def edge_pair(c, k, k0=0):
                edge_weights(c, 2 * k, 2 * k0)
                edge_weights(c, 2 * k + 1, 2 * k0)
                count_edges(c, k, k0)

            def edge_pairs(c, done, until=TP):
                with dve.Fori(0, (until - done) // 3) as kk:
                    for k in range(done, done + 3):
                        edge_pair(c, k, 3 * kk)

            def ask_dis(c):
                dve.wait_ge(deg_psum, c + 1)
                nc.vector.tensor_scalar(pow_in[:, 1, c * R:(c + 1) * R], ps[:, first_bank(c) + 3, 0:R], EDGE,
                                        1.0 / (EDGE * DH_SCALE ** 2), ALU.max, ALU.mult).then_inc(pow_asked, 1)

            def invert_den(c):
                dve.wait_ge(p_used, (c + 1) * T)
                for k, n in BANKS:
                    ins = nc.vector.reciprocal(rden[:, k * BK:k * BK + n], accs(first_bank(c), k, n)[:, :, D])
                pro.link(ins)

            def add_attention(c, rows):
                for r in rows:
                    dst = res[:, c * R + r, :]
                    ins = nc.vector.scalar_tensor_tensor(out=dst, in0=acc(first_bank(c), r, D), scalar=rden[:, r:r + 1],
                                                         in1=dst, op0=ALU.mult, op1=ALU.add)
                if R - 1 in rows:
                    ins.then_inc(acc_free, 1)

            def dis_h_low(q, rows=range(R)):
                dve.wait_ge(dh_hi, q + 1)
                for t in rows:
                    t += q * R
                    ins = nc.vector.scalar_tensor_tensor(out=dh[:, t, 1, :], in0=h1[:, t, :], scalar=dis[:, t:t + 1],
                                                         in1=dh[:, t, 0, :], op0=ALU.mult, op1=ALU.subtract)
                if R - 1 in rows:
                    ins.then_inc(dh_lo, 1)

            low, high = range(R // 2), range(R // 2, R)
            cap_c(0)
            dve.wait_ge(c_ready, 1)
            dve.wait_ge(vg_ready, 2)
            edge_weights(0, 0)
            scale_H(0)
            edge_weights(0, 1)
            scale_H(1)
            edge_pair(0, 1)
            edge_pair(0, 2)
            edge_pair(0, 3)
            for k in range(4, 13, 3):
                scale_H(2 + (k - 4) // 3)
                edge_pairs(0, k, k + 3)
            edge_pairs(0, 13)
            cap_c(1)
            for c in range(1, C):
                dve.wait_ge(c_ready, c + 1)
                edge_weights(c, 0)
                sum_counts(c - 1)
                edge_weights(c, 1)
                edge_pair(c, 1)
                invert_den(c - 1)
                add_attention(c - 1, low)
                edge_pair(c, 2)
                add_attention(c - 1, high)
                edge_pair(c, 3)
                ask_dis(c - 1)
                dve.wait_ge(acc_free, c)
                row_stats(c - 1, low)
                edge_pair(c, 4)
                row_stats(c - 1, high)
                edge_pair(c, 5)
                ask_rstd(c - 1)
                edge_pair(c, 6)
                mean_shift(c - 1, POW_LN1(c - 1))
                if c + 1 < C:
                    cap_c(c + 1)
                    edge_pairs(c, 7)
            edge_pairs(C - 1, THIRD_UNTIL // 2, 13)
            for k in (13, 14):
                for t in (2 * k, 2 * k + 1):
                    edge_weights(C - 1, t)
                    dis_h_low(0, range(2 * (t - 26), 2 * (t - 25)))
                count_edges(C - 1, k)
            edge_pair(C - 1, 15)
            sum_counts(C - 1)

            def widen(c, hf, g, place=None):
                for s in range(ASLOTS // 2):
                    slot, used = a16_slot(c, hf, g, s, place)
                    wait(dve, a16_used, used)
                    nc.vector.tensor_copy(a16[:, slot, :],
                                          adj8[:, c * T + g * ASLOTS + s, hf * HW:(hf + 1) * HW]).then_inc(a16_dve, 1)

            def take_diffusion(chain, c, hf, part):
                dve.wait_ge(a16_used, FIRST_DONE[hf] if isinstance(c, int) and c == 0 else (2 * c + hf + 1) * T)
                for r in range(RH):
                    tile = c * R + hf * RH + r
                    o = (r % 2) * 2 * D + part * D
                    ins = nc.vector.scalar_tensor_tensor(
                        out=row(res, tile), in0=ps[:, 2 * hf + r // 2, o:o + D], scalar=disd[:, bass.ds(tile, 1)],
                        in1=row(res, tile), op0=ALU.mult, op1=ALU.add)
                if part:
                    chain.link(ins)
                else:
                    ins.then_inc(d_free[hf], 1)

            def hnT_low(sub, hf):
                dve.wait_ge(hnT_hi, sub)
                w = bass.ds((sub - 1) * HW, HW)
                nc.vector.tensor_tensor(hnT[:, 1, w], ps[:, 4 + hf, :], hnT[:, 0, w], ALU.subtract).then_inc(hnT_lo, 1)

            def drop_h1(chain, c):
                w = bass.ds(c * R, R)
                chain.link(nc.vector.scalar_tensor_tensor(out=res[:, w, :], in0=h1[:, w, :], scalar=col(C_MSIG),
                                                          in1=res[:, w, :], op0=ALU.mult, op1=ALU.add))

            def split_h1(chain, c):
                w = bass.ds(c * R, R)
                dve.wait_ge(hp_hi, c + 1)
                chain.link(nc.vector.scalar_tensor_tensor(out=hparts[:, 1, :, :], in0=h1[:, w, :], scalar=H_SCALE,
                                                          in1=hparts[:, 0, :, :], op0=ALU.mult, op1=ALU.subtract))

            def place_hp(c):
                w = bass.ds(c * R, R)
                nc.vector.tensor_copy(hp[:, w, D], hcol[:, :])
                nc.vector.tensor_copy(hp[:, w, 0:D], hparts[:, 0, :, :])
                nc.vector.tensor_copy(hp[:, w, A:A + D], hparts[:, 1, :, :]).then_inc(hp_ready, 1)

            def beside_diffusion(chain, c, hf):
                sub = 2 * c + hf
                for g in range(T // ASLOTS):
                    widen(c, hf, g)
                    if g == 1:
                        hnT_low(sub, 1 - hf)
                    if g == 2:
                        take_diffusion(chain, c - 1 + hf, 1 - hf, 1)
                    if g == 3:
                        take_diffusion(chain, c - 1 + hf, 1 - hf, 0)
                    if g == 4 and hf == 0:
                        drop_h1(chain, c)
                    if g == 5 and (hf == 0 or last(c)):
                        split_h1(chain, c if hf else c - 1)
                    if g == 6 and (hf == 0 or last(c)):
                        place_hp(c if hf else c - 1)

            def ask_norms(which, w):
                dve.wait_ge(ssq_ready, C - 1 + which)
                nc.vector.tensor_scalar(pow_in[:, 2, w], ssq[:, w], COS_EPS ** 2, 1.0 / HN_SCALE ** 2,
                                        ALU.max, ALU.mult).then_inc(pow_asked, 1)

            for place, (hf, g) in enumerate(FIRST_GROUPS):
                if place < 2:
                    dve.wait_ge(p_used, NT - 1 + place)
                widen(0, hf, g, place)
                if place == 0:
                    dis_h_low(1)
                if place == 1:
                    invert_den(C - 1)
                    add_attention(C - 1, low)
                if place == 2:
                    ask_dis(C - 1)
                    add_attention(C - 1, high)
                if place == 3:
                    dve.wait_ge(acc_free, C)
                    row_stats(C - 1, range(R))
                if place == 4:
                    ask_rstd(C - 1)
                    ask_norms(0, slice(0, T - R))
                if place == 5:
                    dis_h_low(2, low)
                    mean_shift(C - 1, POW_LN1(C - 1))
                if place == 6:
                    dis_h_low(2, high)
                if place == 7:
                    pro.link(nc.vector.tensor_scalar(disd[:, :], dis[:, :], 1.0 / (EDGE * DH_SCALE ** 2), None,
                                                     ALU.mult))
                    drop_h1(pro, 0)
                if place == 9:
                    dis_h_low(C - 1)
                if place == 11:
                    ask_norms(1, slice(T - R, T))
            hnT_low(1, 0)
            take_diffusion(pro, 0, 0, 1)
            take_diffusion(pro, 0, 0, 0)
            with dve.Fori(1, C - 1) as c:
                chain = Chain(d_step, (c - 1) * 4)
                beside_diffusion(chain, c, 0)
                beside_diffusion(chain, c, 1)
            beside_diffusion(pro, C - 1, 0)
            beside_diffusion(pro, C - 1, 1)
            hnT_low(2 * C, 1)
            take_diffusion(pro, C - 1, 1, 1)
            take_diffusion(pro, C - 1, 1, 0)

            def mask(n, par):
                dve.wait_ge(q_ready, n + 1)
                wait(dve, ylo_ready, n - 1)
                nc.vector.scalar_tensor_tensor(out=wt[:, par, :], in0=area(par), scalar=col(C_E0),
                                               in1=adj8[:, n, :], op0=ALU.subtract, op1=ALU.mult).then_inc(y_ready, 1)

            def y_low(n, par):
                dve.wait_ge(yhi_ready, n + 1)
                nc.vector.scalar_tensor_tensor(out=yp[:, par, 1, :], in0=wt[:, par, :], scalar=Y_SCALE,
                                               in1=yp[:, par, 0, :], op0=ALU.mult,
                                               op1=ALU.subtract).then_inc(ylo_ready, 1)

            def take_sums(c):
                dve.wait_ge(out_ready, c)
                for k, n in BANKS:
                    if k < len(BANKS) - 1:
                        dve.wait_ge(sums_ready, c * (len(BANKS) - 1) + k + 1)
                    else:
                        dve.wait_ge(y_used, (c + 1) * T)
                    ins = nc.vector.tensor_tensor(fin[:, k * BK:k * BK + n, :], accs(4, k, n),
                                                  tot[:, :].unsqueeze(1).broadcast_to([P, n, A]), ALU.add)
                pro.link(ins)

            def add_tot(c, rows):
                dve.wait_ge(sums_kept, (c + 1) * len(BANKS))
                w = slice(rows[0], rows[-1] + 1)
                pro.link(nc.vector.tensor_tensor(fin[:, w, :], fin[:, w, :],
                                                 tot[:, :].unsqueeze(1).broadcast_to([P, len(rows), A]), ALU.add))

            def invert_sums():
                pro.link(nc.vector.reciprocal(rden[:, :], fin[:, :, D]))
                pro.link(nc.vector.tensor_scalar(rden[:, :], rden[:, :], col(C_SIG), None, ALU.mult))

            def finish(c, rows):
                for r in rows:
                    dst = res[:, c * R + r, :]
                    ins = nc.vector.scalar_tensor_tensor(out=dst, in0=fin[:, r, 0:D], scalar=rden[:, r:r + 1],
                                                         in1=dst, op0=ALU.mult, op1=ALU.add)
                if R - 1 in rows or c == C - 1:
                    ins.then_inc(out_ready, 1)

            def mask_pair(k):
                mask(2 * k + 1, 1)
                y_low(2 * k, 0)
                mask(2 * k + 2, 0)
                y_low(2 * k + 1, 1)

            dve.wait_ge(scal_ready, 2)
            mask(0, 0)
            mask_pair(0)
            dve.wait_ge(tot_psum, 1)
            nc.vector.tensor_scalar(tot[:, :], ps[:, 7, 0:A], col(C_E0), EDGE * Y_SCALE, ALU.mult, ALU.mult)
            mask_pair(1)
            for hf in range(2):
                dve.wait_ge(d_free[hf], C)
            for c in range(C):
                done = 2
                if c >= 1:
                    mask_pair(c * TP)
                    mask_pair(c * TP + 1)
                    add_tot(c - 1, low)
                    mask_pair(c * TP + 2)
                    add_tot(c - 1, high)
                    mask_pair(c * TP + 3)
                    invert_sums()
                    done = 4
                    for r in range(0, R, 2):
                        mask_pair(c * TP + done)
                        finish(c - 1, range(r, r + 2))
                        done += 1
                with dve.Fori(c * TP + done, (c + 1) * TP - (c == C - 1)) as k:
                    mask_pair(k)
            mask(NT - 1, 1)
            y_low(NT - 2, 0)
            y_low(NT - 1, 1)
            take_sums(C - 1)
            invert_sums()
            finish(C - 1, low)
            finish(C - 1, high)


def kernel(**inputs):
    import numpy as _np
    import concourse.bacc as _bacc
    from concourse import mybir as _mybir
    from concourse.bass_utils import run_bass_kernel_spmd as _run

    x = _np.ascontiguousarray(inputs["x"])
    n = x.shape[1]
    b = _np.asarray(inputs["L0_gnn_b"])
    W = _np.asarray(inputs["L0_gnn_W"])
    a_s = _np.asarray(inputs["L0_gnn_a_s"])
    columns = [W, _np.broadcast_to(a_s, (n, n)), _np.broadcast_to(b[:, None], (n, n)),
               _np.asarray(inputs["L0_gnn_a_r"]), a_s,
               _np.broadcast_to(_np.asarray(inputs["L1_gnn_alpha"]), (n, 1)),
               _np.broadcast_to(_np.asarray(inputs["L1_gnn_beta"]), (n, 1)),
               _np.broadcast_to(b[None, :], (n, n))]
    arrays = {"x": x, "adjT": _np.asarray(inputs["adj"]).T, "WT": W.T, "params": _np.concatenate(columns, axis=1)}
    arrays = {k: _np.ascontiguousarray(v) for k, v in arrays.items()}
    nc = _bacc.Bacc("TRN2", target_bir_lowering=False, num_devices=1)
    args = [nc.dram_tensor(k, v.shape, _mybir.dt.from_np(v.dtype), kind="ExternalInput").ap()
            for k, v in arrays.items()]
    args.append(nc.dram_tensor("out", x.shape, _mybir.dt.from_np(x.dtype), kind="ExternalOutput").ap())
    gat_then_cosine_diffusion(nc, *args)
    r = _run(nc, [arrays], core_ids=[0])
    return r.results[0]["out"]
```
